# Optimizing a Trainium2 kernel written in Bass

```python
import numpy as np
import jax
import jax.numpy as jnp

def _softmax(x, axis=-1):
    return jax.nn.softmax(x, axis=axis)

def _gelu(x):
    return jax.nn.gelu(x, approximate=True)

def _silu(x):
    return jax.nn.silu(x)

def _sigmoid(x):
    return jax.nn.sigmoid(x)

def _layernorm(x, axis=-1, eps=1e-05):
    m = jnp.mean(x, axis=axis, keepdims=True)
    v = jnp.var(x, axis=axis, keepdims=True)
    return (x - m) / jnp.sqrt(v + eps)

def _scatter_add(tgt, idx, src, axis=0):
    return tgt.at[idx].add(src)

def _segment_sum(src, seg, n):
    return jax.ops.segment_sum(src, seg, n)
kernel_name = 'mk_flamingo_gated_d2_seqx_r8_33f818'

def setup_inputs(seed: int=0):
    np.random.seed(seed)
    _w = jnp.asarray

    def _rec_inputs():
        import jax
        import jax.numpy as jnp
        _rk = jax.random.key(seed)
        x = -0.0005207 + 1.001 * jax.random.normal(jax.random.fold_in(_rk, 1), (64, 64, 128), jnp.float32)
        _lenS = 64 - jax.random.randint(jax.random.fold_in(_rk, 7), (64,), 0, max(1, 64 // 4) + 1, jnp.int32)
        _lenS2 = 64 - jax.random.randint(jax.random.fold_in(_rk, 8), (64,), 0, max(1, 64 // 4) + 1, jnp.int32)
        _ctx_1024P = jax.random.normal(jax.random.fold_in(_rk, 11), (64, 16, 128), jnp.float32)
        _ctx_1024c = jax.random.dirichlet(jax.random.fold_in(_rk, 511), 0.3 * jnp.ones((16,), jnp.float32), (64, 64))
        _ctx_1024t = jnp.einsum('bsk,bkd->bsd', _ctx_1024c, _ctx_1024P)
        _ctx_1024t = _ctx_1024t * jax.lax.rsqrt(jnp.mean(jnp.square(_ctx_1024t)) + 1e-12) * 0.953939
        ctx_1024 = -0.000514642 + 1.00011 * (_ctx_1024t + 0.3 * jax.random.normal(jax.random.fold_in(_rk, 611), (64, 64, 128), jnp.float32))
        _g = jax.random.normal(jax.random.fold_in(_rk, 9001), (2, 2), jnp.float32)
        _g = jnp.sign(_g) * jnp.maximum(jnp.abs(_g), 1.0) + (_g == 0) * 1.0
        g_xattn = _g[0]
        g_ffn = _g[1]
        return (x, ctx_1024, g_xattn, g_ffn)
    x, ctx_1024, g_xattn, g_ffn = _rec_inputs()

    def _L0_xattn_setup():
        import jax, jax.numpy as jnp
        import numpy as np
        D_MODEL = 128
        FFN = 512
        E = 8
        K = 2
        B, S = (4, 64)
        key = jax.random.key(seed)
        ks = jax.random.split(key, 8)
        scale_in = 1.0 / np.sqrt(D_MODEL)
        scale_ffn = 1.0 / np.sqrt(FFN)
        return {'x': jax.random.normal(ks[0], (B, S, D_MODEL), jnp.float32), 'context': jax.random.normal(ks[1], (B, S, D_MODEL), jnp.float32), 'Wg': jax.random.normal(ks[2], (D_MODEL, E), jnp.float32) * scale_in, 'bg': jnp.zeros((E,), jnp.float32), 'W1': jax.random.normal(ks[3], (E, D_MODEL, FFN), jnp.float32) * scale_in, 'b1': jnp.zeros((E, FFN), jnp.float32), 'W2': jax.random.normal(ks[4], (E, FFN, D_MODEL), jnp.float32) * scale_ffn, 'b2': jnp.zeros((E, D_MODEL), jnp.float32)}
    _L0_xattn_all = _L0_xattn_setup()
    _L0_xattn_in = {k: v for k, v in _L0_xattn_all.items() if k in ('Wg', 'bg', 'W1', 'b1', 'W2', 'b2')}
    del _L0_xattn_all

    def _L0_ffn_setup():
        import jax, jax.numpy as jnp
        import numpy as np
        E = 32
        H = 128
        I = 64
        G = 8
        TKG = 4
        TOPK = 8
        NSH = 2
        SCALE = 2.5
        key = jax.random.key(seed)
        ks = jax.random.split(key, 10)
        s = 0.02
        return {'hidden_states': jax.random.normal(ks[0], (2, 128, H), jnp.float32), 'gate_w': jax.random.normal(ks[1], (E, H), jnp.float32) * s, 'gate_bias': jax.random.normal(ks[2], (E,), jnp.float32) * s, 'w_gate': jax.random.normal(ks[3], (E, I, H), jnp.float32) * s, 'w_up': jax.random.normal(ks[4], (E, I, H), jnp.float32) * s, 'w_down': jax.random.normal(ks[5], (E, H, I), jnp.float32) * s, 'sh_gate': jax.random.normal(ks[6], (I * NSH, H), jnp.float32) * s, 'sh_up': jax.random.normal(ks[7], (I * NSH, H), jnp.float32) * s, 'sh_down': jax.random.normal(ks[8], (H, I * NSH), jnp.float32) * s}
    _L0_ffn_all = _L0_ffn_setup()
    _L0_ffn_in = {k: v for k, v in _L0_ffn_all.items() if k in ('gate_w', 'gate_bias', 'w_gate', 'w_up', 'w_down', 'sh_gate', 'sh_up', 'sh_down')}
    del _L0_ffn_all

    def _L1_xattn_setup():
        import jax, jax.numpy as jnp
        import numpy as np
        D_MODEL = 128
        N_HEADS = 16
        D_K = D_MODEL // N_HEADS
        key = jax.random.key(seed)
        ks = jax.random.split(key, 11)
        B, L, S = (2, 256, 256)
        scale = 1.0 / np.sqrt(D_MODEL)
        return {'x_q': jax.random.normal(ks[0], (B, L, D_MODEL), jnp.float32), 'x_k': jax.random.normal(ks[1], (B, S, D_MODEL), jnp.float32), 'x_v': jax.random.normal(ks[2], (B, S, D_MODEL), jnp.float32), 'W_Q': jax.random.normal(ks[3], (D_MODEL, D_MODEL), jnp.float32) * scale, 'b_Q': jax.random.normal(ks[4], (D_MODEL,), jnp.float32) * 0.01, 'W_K': jax.random.normal(ks[5], (D_MODEL, D_MODEL), jnp.float32) * scale, 'b_K': jax.random.normal(ks[6], (D_MODEL,), jnp.float32) * 0.01, 'W_V': jax.random.normal(ks[7], (D_MODEL, D_MODEL), jnp.float32) * scale, 'b_V': jax.random.normal(ks[8], (D_MODEL,), jnp.float32) * 0.01, 'W_O': jax.random.normal(ks[9], (D_MODEL, D_MODEL), jnp.float32) * scale, 'b_O': jax.random.normal(ks[10], (D_MODEL,), jnp.float32) * 0.01}
    _L1_xattn_all = _L1_xattn_setup()
    _L1_xattn_in = {k: v for k, v in _L1_xattn_all.items() if k in ('W_Q', 'b_Q', 'W_K', 'b_K', 'W_V', 'b_V', 'W_O', 'b_O')}
    del _L1_xattn_all

    def _L1_ffn_setup():
        import jax, jax.numpy as jnp
        import numpy as np
        EMB = 128
        FF = 4 * EMB

        def _ternary(w):
            scale = jnp.maximum(jnp.mean(jnp.abs(w)), 1e-08)
            w_t = jnp.clip(jnp.round(w / scale), -1.0, 1.0)
            return w + jax.lax.stop_gradient(w_t - w)
        key = jax.random.key(seed)
        kx, k1, k2, kb1, kb2 = jax.random.split(key, 5)
        x = jax.random.normal(kx, (4, 256, EMB), dtype=jnp.float32)
        lim1 = 1.0 / np.sqrt(EMB)
        lim2 = 1.0 / np.sqrt(FF)
        W1 = jax.random.uniform(k1, (FF, EMB), jnp.float32, -lim1, lim1)
        b1 = jax.random.uniform(kb1, (FF,), jnp.float32, -lim1, lim1)
        W2 = jax.random.uniform(k2, (EMB, FF), jnp.float32, -lim2, lim2)
        b2 = jax.random.uniform(kb2, (EMB,), jnp.float32, -lim2, lim2)
        return {'x': x, 'W1': W1, 'b1': b1, 'W2': W2, 'b2': b2}
    _L1_ffn_all = _L1_ffn_setup()
    _L1_ffn_in = {k: v for k, v in _L1_ffn_all.items() if k in ('W1', 'b1', 'W2', 'b2')}
    del _L1_ffn_all
    return {'x': x, 'ctx_1024': ctx_1024, 'g_xattn': g_xattn, 'g_ffn': g_ffn, 'L0_xattn_Wg': _L0_xattn_in['Wg'], 'L0_xattn_bg': _L0_xattn_in['bg'], 'L0_xattn_W1': _L0_xattn_in['W1'], 'L0_xattn_b1': _L0_xattn_in['b1'], 'L0_xattn_W2': _L0_xattn_in['W2'], 'L0_xattn_b2': _L0_xattn_in['b2'], 'L0_ffn_gate_w': _L0_ffn_in['gate_w'], 'L0_ffn_gate_bias': _L0_ffn_in['gate_bias'], 'L0_ffn_w_gate': _L0_ffn_in['w_gate'], 'L0_ffn_w_up': _L0_ffn_in['w_up'], 'L0_ffn_w_down': _L0_ffn_in['w_down'], 'L0_ffn_sh_gate': _L0_ffn_in['sh_gate'], 'L0_ffn_sh_up': _L0_ffn_in['sh_up'], 'L0_ffn_sh_down': _L0_ffn_in['sh_down'], 'L1_xattn_W_Q': _L1_xattn_in['W_Q'], 'L1_xattn_b_Q': _L1_xattn_in['b_Q'], 'L1_xattn_W_K': _L1_xattn_in['W_K'], 'L1_xattn_b_K': _L1_xattn_in['b_K'], 'L1_xattn_W_V': _L1_xattn_in['W_V'], 'L1_xattn_b_V': _L1_xattn_in['b_V'], 'L1_xattn_W_O': _L1_xattn_in['W_O'], 'L1_xattn_b_O': _L1_xattn_in['b_O'], 'L1_ffn_W1': _L1_ffn_in['W1'], 'L1_ffn_b1': _L1_ffn_in['b1'], 'L1_ffn_W2': _L1_ffn_in['W2'], 'L1_ffn_b2': _L1_ffn_in['b2']}

def reference(x, ctx_1024, g_xattn, g_ffn, L0_xattn_Wg, L0_xattn_bg, L0_xattn_W1, L0_xattn_b1, L0_xattn_W2, L0_xattn_b2, L0_ffn_gate_w, L0_ffn_gate_bias, L0_ffn_w_gate, L0_ffn_w_up, L0_ffn_w_down, L0_ffn_sh_gate, L0_ffn_sh_up, L0_ffn_sh_down, L1_xattn_W_Q, L1_xattn_b_Q, L1_xattn_W_K, L1_xattn_b_K, L1_xattn_W_V, L1_xattn_b_V, L1_xattn_W_O, L1_xattn_b_O, L1_ffn_W1, L1_ffn_b1, L1_ffn_W2, L1_ffn_b2):
    import jax
    import jax.numpy as jnp

    def _L0_xattn_ref(x, context, Wg, bg, W1, b1, W2, b2):
        import jax, jax.numpy as jnp
        import numpy as np
        D_MODEL = 128
        FFN = 512
        E = 8
        K = 2
        B, S = (4, 64)
        logits = jnp.einsum('bsd,de->bse', context, Wg) + bg
        scores_topk, idx_topk = jax.lax.top_k(logits, K)
        weights = jax.nn.softmax(scores_topk, axis=-1)
        combine = jnp.sum(jax.nn.one_hot(idx_topk, E, dtype=weights.dtype) * weights[..., None], axis=-2)
        h = jax.nn.relu(jnp.einsum('bsd,edf->bsef', x, W1) + b1)
        y = jnp.einsum('bsef,efd->bsed', h, W2) + b2
        out = jnp.einsum('bsed,bse->bsd', y, combine)
        return out

    def _L0_ffn_ref(hidden_states, gate_w, gate_bias, w_gate, w_up, w_down, sh_gate, sh_up, sh_down):
        import jax, jax.numpy as jnp
        import numpy as np
        E = 32
        H = 128
        I = 64
        G = 8
        TKG = 4
        TOPK = 8
        NSH = 2
        SCALE = 2.5
        B, S, Hd = hidden_states.shape
        h = hidden_states.reshape(-1, Hd)
        logits = h.astype(jnp.float32) @ gate_w.T
        scores = jax.nn.sigmoid(logits)
        sc = scores + gate_bias
        grp = sc.reshape(-1, G, E // G)
        group_scores = jax.lax.top_k(grp, 2)[0].sum(-1)
        gidx = jax.lax.top_k(group_scores, TKG)[1]
        gmask = jnp.sum(jax.nn.one_hot(gidx, G, dtype=sc.dtype), axis=1)
        smask = jnp.repeat(gmask, E // G, axis=1)
        masked = jnp.where(smask > 0, sc, jnp.zeros_like(sc))
        tki = jax.lax.top_k(masked, TOPK)[1]
        tkw = jnp.take_along_axis(scores, tki, axis=1)
        tkw = tkw / (tkw.sum(-1, keepdims=True) + 1e-20)
        tkw = tkw * SCALE
        combine = (jax.nn.one_hot(tki, E, dtype=tkw.dtype) * tkw[..., None]).sum(1)
        g = jax.nn.silu(jnp.einsum('th,eih->tei', h, w_gate))
        u = jnp.einsum('th,eih->tei', h, w_up)
        routed = jnp.einsum('tei,ehi->th', g * u * combine[:, :, None], w_down)
        sg = jax.nn.silu(h @ sh_gate.T)
        shared = sg * (h @ sh_up.T) @ sh_down.T
        return (routed + shared).reshape(B, S, Hd)

    def _L1_xattn_ref(x_q, x_k, x_v, W_Q, b_Q, W_K, b_K, W_V, b_V, W_O, b_O):
        import jax, jax.numpy as jnp
        import numpy as np
        D_MODEL = 128
        N_HEADS = 16
        D_K = D_MODEL // N_HEADS
        B, L, _ = x_q.shape
        S = x_k.shape[1]
        H, dk = (N_HEADS, D_K)
        Q = (x_q @ W_Q + b_Q).reshape(B, L, H, dk).transpose(0, 2, 1, 3)
        K = (x_k @ W_K + b_K).reshape(B, S, H, dk).transpose(0, 2, 1, 3)
        V = (x_v @ W_V + b_V).reshape(B, S, H, dk).transpose(0, 2, 1, 3)
        scores = jnp.einsum('bhld,bhsd->bhls', Q, K) / jnp.sqrt(jnp.float32(dk))
        attn = jax.nn.softmax(scores, axis=-1)
        ctx = jnp.einsum('bhls,bhsd->bhld', attn, V)
        ctx = ctx.transpose(0, 2, 1, 3).reshape(B, L, H * dk)
        out = ctx @ W_O + b_O
        return out

    def _L1_ffn_ref(x, W1, b1, W2, b2):
        import jax, jax.numpy as jnp
        import numpy as np
        EMB = 128
        FF = 4 * EMB

        def _ternary(w):
            scale = jnp.maximum(jnp.mean(jnp.abs(w)), 1e-08)
            w_t = jnp.clip(jnp.round(w / scale), -1.0, 1.0)
            return w + jax.lax.stop_gradient(w_t - w)
        h = jnp.einsum('bsd,fd->bsf', x, _ternary(W1)) + b1
        h = jax.nn.gelu(h, approximate=False)
        out = jnp.einsum('bsf,df->bsd', h, _ternary(W2)) + b2
        return out
    x = x + jnp.tanh(g_xattn[0]) * _L0_xattn_ref(_layernorm(x, axis=-1), ctx_1024, L0_xattn_Wg, L0_xattn_bg, L0_xattn_W1, L0_xattn_b1, L0_xattn_W2, L0_xattn_b2)
    x = x + jnp.tanh(g_ffn[0]) * _L0_ffn_ref(_layernorm(x, axis=-1), L0_ffn_gate_w, L0_ffn_gate_bias, L0_ffn_w_gate, L0_ffn_w_up, L0_ffn_w_down, L0_ffn_sh_gate, L0_ffn_sh_up, L0_ffn_sh_down)
    x = x + jnp.tanh(g_xattn[1]) * _L1_xattn_ref(_layernorm(x, axis=-1), ctx_1024, ctx_1024, L1_xattn_W_Q, L1_xattn_b_Q, L1_xattn_W_K, L1_xattn_b_K, L1_xattn_W_V, L1_xattn_b_V, L1_xattn_W_O, L1_xattn_b_O)
    x = x + jnp.tanh(g_ffn[1]) * _L1_ffn_ref(_layernorm(x, axis=-1), L1_ffn_W1, L1_ffn_b1, L1_ffn_W2, L1_ffn_b2)
    return x

_drawn_inputs = setup_inputs


def setup_inputs(seed=0):
    import zlib

    import numpy as np

    out = dict(_drawn_inputs(seed))
    spreads = {'g_ffn': (-1.0, 0.2),
     'L0_xattn_bg': (0.0, 0.1),
     'L0_xattn_b1': (0.0, 0.1),
     'L0_xattn_b2': (0.0, 0.1)}
    factors = {'L0_ffn_gate_w': 8.0,
     'L0_ffn_gate_bias': 8.0,
     'L0_ffn_w_gate': 8.0,
     'L0_ffn_w_up': 8.0,
     'L0_ffn_w_down': 8.0,
     'L0_ffn_sh_gate': 8.0,
     'L0_ffn_sh_up': 8.0,
     'L0_ffn_sh_down': 8.0,
     'L1_xattn_b_Q': 64.0,
     'L1_xattn_b_K': 200.0,
     'L1_xattn_b_V': 19.247,
     'L1_xattn_b_O': 17.778,
     'L1_ffn_b1': 8.0,
     'L1_ffn_b2': 200.0}
    for name, (base, spread) in spreads.items():
        noise = np.random.default_rng([zlib.crc32(name.encode()), seed]).standard_normal(out[name].shape)
        drawn = base * np.exp(spread * noise) if base else spread * noise
        out[name] = jnp.asarray(drawn.astype(out[name].dtype))
    for name, factor in factors.items():
        out[name] = (out[name] * factor).astype(out[name].dtype)
    return out
```

```python
from contextlib import ExitStack

import concourse.bass as bass
from concourse import mybir

F32 = mybir.dt.float32
F16 = mybir.dt.float16
ALU = mybir.AluOpType
ACT = mybir.ActivationFunctionType
AX = mybir.AxisListType

P = 128
CT = 512
JT = CT // P
WSCALE = 64.0
EPS = 1e-5
SEQ = 64
HEADS, DK = 16, 8
ROUTED_SCALE = 2.5


class Chain:

    def __init__(self, eng, sem):
        self.eng, self.sem, self.n = eng, sem, 0

    def __call__(self, ins):
        ins.then_inc(self.sem, 1)
        self.n += 1
        return ins

    def sync(self):
        self.eng.wait_ge(self.sem, self.n)

    def restart(self):
        if self.n:
            self.sync()
        self.eng.sem_clear(self.sem)
        self.n = 0


def at_least(eng, sem, count):
    if isinstance(count, int) and count <= 0:
        return
    eng.wait_ge(sem, count)


class Norm:

    def __init__(self, name, sb, sem):
        self.stats = sb(name + "_stats", [P, JT, 6], F32)
        self.mean_var = sb(name + "_mean_var", [P, JT, 2], F32)
        self.var_eps = sb(name + "_var_eps", [P, JT], F32)
        self.rstd = sb(name + "_rstd", [P, JT], F32)
        self.xn = sb(name + "_xn", [P, JT, P], F32)
        self.hi = sb(name + "_hi", [P, CT], F16)
        self.lo = sb(name + "_lo", [P, CT], F16)
        self.var_ready = sem(name + "_var_ready")
        self.rstd_ready = sem(name + "_rstd_ready")
        self.xn_ready = sem(name + "_xn_ready")
        self.xT_ready = sem(name + "_xT_ready")
        self.hi_ready = sem(name + "_hi_ready")
        self.lo_ready = sem(name + "_lo_ready")


def build_flamingo(nc, x_d, ctxT_d, g_xattn_d, g_ffn_d, wg_d, bg_d, w1_d, b1_d, w2_d, b2_d,
                   gate_w_d, gate_bias_d, w_gate_d, w_up_d, w_down_d, sh_gate_d, sh_up_d, sh_down_d,
                   wq_d, bq_d, wk_d, bk_d, wv_d, bv_d, wo_d, bo_d, f1_d, fb1_d, f2_d, fb2_d, out_d):
    T = x_d.shape[0]
    NT, NC = T // P, T // CT
    E8, FC = 8, 4
    E32, PAIRS = 32, 16
    NP = PAIRS + 1
    GROUPS, PER_GROUP, TOP_GROUPS = 8, 4, 4
    NB = CT // SEQ
    BP = NB // 2
    V9 = DK + 1

    with ExitStack() as ctx:
        def sb(name, shape, dt):
            return ctx.enter_context(nc.sbuf_tensor(name, shape, dt))

        def sem(name):
            return ctx.enter_context(nc.semaphore(name))

        x_sb = sb("x_sb", [P, NT, P], F32)
        w1 = sb("w1", [P, 2, E8 * FC * P], F16)
        w2 = sb("w2", [P, 2, E8 * FC * P], F16)
        wgu_g = sb("wgu_g", [P, 2, NP * P], F16)
        wgu_u = sb("wgu_u", [P, 2, NP * P], F16)
        wdn = sb("wdn", [P, 2, NP * P], F16)
        watt = sb("watt", [P, 2, 4 * P], F16)
        wgate = sb("wgate", [P, 2, E8 + E32], F16)
        wt1 = sb("wt1", [P, FC * P], F16)
        wt2 = sb("wt2", [P, FC * P], F16)
        b2s = sb("b2s", [1, 2, E8 * P], F16)
        stage = sb("stage", [P, 2, 2048], F32)
        tern = sb("tern", [P, 2, FC * P], F32)
        tern_neg = sb("tern_neg", [P, 2, FC * P], F32)
        b1T = sb("b1T", [P, E8 * FC], F32)
        b2row = sb("b2row", [1, E8 * P], F32)
        bg_bc = sb("bg_bc", [P, E8], F32)
        gbias_bc = sb("gbias_bc", [P, JT, E32], F32)
        bq_col = sb("bq_col", [P, 1], F32)
        bqs_col = sb("bqs_col", [P, 1], F32)
        bk_col = sb("bk_col", [P, 1], F32)
        bv_bc = sb("bv_bc", [P, P], F32)
        bv8 = sb("bv8", [P, NB * SEQ], F32)
        bo4 = sb("bo4", [P, JT, P], F32)
        fb1_col = sb("fb1_col", [P, FC], F32)
        fb2_4 = sb("fb2_4", [P, JT, P], F32)
        gates = sb("gates", [P, 4], F32)
        tg = sb("tg", [P, 4], F32)
        tgs = sb("tgs", [P, 4], F32)
        ident = sb("ident", [P, P], F32)
        ones = sb("ones", [P, P], F32)
        ones16 = sb("ones16", [1, CT], F16)
        unscale16 = sb("unscale16", [1, P], F16)
        tri = sb("tri", [P, 8, 8], F32)
        hm = sb("hm", [P, 4, 4], F32)
        headmask = sb("headmask", [P, 4], F32)
        sel = sb("sel", [2 * E32, PAIRS, 2, SEQ], F16)
        half_pow = sb("half_pow", [P, JT], F32)
        tern_sum = sb("tern_sum", [P, 2], F32)
        tern_hs = sb("tern_hs", [P, 2], F32)
        tern_nhs = sb("tern_nhs", [P, 2], F32)

        staged = [sem("staged0"), sem("staged1")]
        split_hi_done = sem("split_hi_done")
        split_lo_done = sem("split_lo_done")
        small_loaded = sem("small_loaded")
        x_loaded = sem("x_loaded")
        tern_loaded = sem("tern_loaded")
        const_ready = sem("const_ready")
        pool_step = sem("pool_step")
        tern_abs_ready = sem("tern_abs_ready")
        tern_total_ready = sem("tern_total_ready")
        tern_ready = sem("tern_ready")
        tanh_ready = sem("tanh_ready")
        tgs_ready = sem("tgs_ready")
        dve_chain = sem("dve_chain")
        act_chain = sem("act_chain")

        nA, nB, nC, nD = (Norm(n, sb, sem) for n in ("A", "B", "C", "D"))
        cx = {}
        for s in ("A", "C"):
            cx[s] = dict(f=sb(f"cx{s}_f", [P, CT], F32), hi=sb(f"cx{s}_hi", [P, CT], F16),
                         lo=sb(f"cx{s}_lo", [P, CT], F16), loaded=sem(f"cx{s}_loaded"),
                         hi_ready=sem(f"cx{s}_hi_ready"), lo_ready=sem(f"cx{s}_lo_ready"))
        a_logits = sb("a_logits", [P, JT, E8], F32)
        rk_gt = sb("rk_gt", [P, JT, 8, 8], F32)
        rk_eq = sb("rk_eq", [P, JT, 8, 8], F32)
        rk = sb("rk", [P, JT, 8], F32)
        a_max = sb("a_max", [P, JT], F32)
        a_sum = sb("a_sum", [P, JT], F32)
        a_rec = sb("a_rec", [P, JT], F32)
        a_exp = sb("a_exp", [P, JT, E8], F32)
        a_w = sb("a_w", [P, JT, E8], F32)
        a_r = sb("a_r", [P, 4, CT], F32)
        halves = stage[:, :, :].bitcast(F16).rearrange("p h (b k t) -> p h b k t", b=2, k=FC)
        a_hh, a_hl = halves[:, 0], halves[:, 1]
        a_acc = sb("a_acc", [P, JT, P], F32)
        a_logit_ready = sem("a_logit_ready")
        a_shift_ready = sem("a_shift_ready")
        a_exp_ready = sem("a_exp_ready")
        a_h_ready = sem("a_h_ready")
        a_hi_ready = sem("a_hi_ready")
        a_lo_ready = sem("a_lo_ready")
        a_y_ready = sem("a_y_ready")
        a_y_used = sem("a_y_used")
        a_x_done = sem("a_x_done")

        b_th = sb("b_th", [P, JT * E32], F32)
        b_sc = sb("b_sc", [P, JT, E32], F32)
        b_scb = sb("b_scb", [P, JT * GROUPS, 2, 2], F32)
        b_mx = sb("b_mx", [P, JT * GROUPS, 2], F32)
        b_mn = sb("b_mn", [P, JT * GROUPS, 2], F32)
        b_t1 = sb("b_t1", [P, JT * GROUPS], F32)
        b_t2 = sb("b_t2", [P, JT * GROUPS], F32)
        b_t3 = sb("b_t3", [P, JT * GROUPS], F32)
        b_gs = sb("b_gs", [P, JT, GROUPS], F32)
        b_gm = sb("b_gm", [P, JT, GROUPS], F32)
        b_masked = sb("b_masked", [P, JT, E32], F32)
        b_m8 = sb("b_m8", [P, JT, 8], F32)
        b_mr = sb("b_mr", [P, JT, E32], F32)
        b_ws = sb("b_ws", [P, JT, E32], F32)
        b_wsum = sb("b_wsum", [P, JT], F32)
        b_wrec = sb("b_wrec", [P, JT], F32)
        b_comb = sb("b_comb", [P, JT, E32], F32)
        b_cT = sb("b_cT", [2 * E32, CT], F16)
        b_silu = sb("b_silu", [P, 2, CT], F32)
        b_su = sb("b_su", [P, 2, CT], F32)
        b_act = sb("b_act", [P, 2, CT], F32)
        b_ah = sb("b_ah", [P, 3, CT], F16)
        b_al = sb("b_al", [P, 3, CT], F16)
        b_yT = sb("b_yT", [P, CT], F32)
        b_route_ready = sem("b_route_ready")
        b_score_ready = sem("b_score_ready")
        b_comb_ready = sem("b_comb_ready")
        b_combT_ready = sem("b_combT_ready")
        b_ch_ready = sem("b_ch_ready")
        b_cl_ready = sem("b_cl_ready")
        b_g_ready = sem("b_g_ready")
        b_gu_ready = sem("b_gu_ready")
        b_silu_ready = sem("b_silu_ready")
        b_u_used = sem("b_u_used")
        b_act_ready = sem("b_act_ready")
        b_ah_ready = sem("b_ah_ready")
        b_al_ready = sem("b_al_ready")
        b_down_done = sem("b_down_done")
        b_yT_ready = sem("b_yT_ready")
        b_y_ready = sem("b_y_ready")
        b_x_done = sem("b_x_done")

        c_q = sb("c_q", [P, CT], F32)
        c_qh = sb("c_qh", [P, CT], F16)
        c_ql = sb("c_ql", [P, CT], F16)
        c_k = sb("c_k", [P, CT], F32)
        c_kh = sb("c_kh", [P, CT], F16)
        c_kl = sb("c_kl", [P, CT], F16)
        c_km = sb("c_km", [P, 2, 4, CT], F16)
        c_vbd = sb("c_vbd", [P, NB, HEADS // 2, 2, V9], F32)
        c_max = sb("c_max", [P, HEADS], F32)
        w1_f32 = w1[:, :, :].bitcast(F32)
        c_p = w1_f32[:, 0, :].rearrange("p (b n) -> p b n", b=2)
        c_pT = w1_f32[:, 1, :].rearrange("p (b h t) -> p b h t", b=2, t=P)
        c_rec = sb("c_rec", [P, HEADS], F32)
        c_on = a_r[:, 0, :].rearrange("p (j h k) -> p j h k", h=HEADS, k=DK)
        c_oh, c_ol = tern_neg[:, 0, 0:CT // 2].bitcast(F16), tern_neg[:, 0, CT // 2:].bitcast(F16)
        c_y = a_r[:, 1, :].rearrange("p (j d) -> p j d", d=P)
        c_qp_ready = sem("c_qp_ready")
        c_q_ready = sem("c_q_ready")
        c_ql_ready = sem("c_ql_ready")
        c_kp_ready = sem("c_kp_ready")
        c_k_ready = sem("c_k_ready")
        c_km_ready = sem("c_km_ready")
        c_vp_ready = sem("c_vp_ready")
        c_v_ready = sem("c_v_ready")
        c_s_ready = sem("c_s_ready")
        c_shift_ready = sem("c_shift_ready")
        c_exp_ready = sem("c_exp_ready")
        c_pT_ready = sem("c_pT_ready")
        c_pT_copied = sem("c_pT_copied")
        c_o_ready = sem("c_o_ready")
        c_on_ready = sem("c_on_ready")
        c_oT_ready = sem("c_oT_ready")
        c_oh_ready = sem("c_oh_ready")
        c_ol_ready = sem("c_ol_ready")
        c_y_ready = sem("c_y_ready")
        c_y_used = sem("c_y_used")
        c_x_done = sem("c_x_done")

        d_g = w2[:, 0, :].bitcast(F32).rearrange("p (k t) -> p k t", k=FC)
        d_gh = w2[:, 1, 0:FC * CT].rearrange("p (k t) -> p k t", k=FC)
        d_gl = w2[:, 1, FC * CT:].rearrange("p (k t) -> p k t", k=FC)
        d_y = a_r[:, 2, :].rearrange("p (j d) -> p j d", d=P)
        x_out = a_r[:, 3, :].rearrange("p (j d) -> p j d", d=P)
        d_h_ready = sem("d_h_ready")
        d_g_ready = sem("d_g_ready")
        d_gl_ready = sem("d_gl_ready")
        d_y_ready = sem("d_y_ready")
        d_x_ready = sem("d_x_ready")
        stored = sem("stored")

        ps4 = ctx.enter_context(nc.psum_tensor("ps4", [P, 4, 512], F32))
        ps2 = ctx.enter_context(nc.psum_tensor("ps2", [P, 2, 512], F32))
        ps_out = ctx.enter_context(nc.psum_tensor("ps_out", [P, 512], F32))
        ps_misc = ctx.enter_context(nc.psum_tensor("ps_misc", [P, 512], F32))

        x_dram = x_d.rearrange("(n p) d -> p n d", p=P)
        out_dram = out_d.rearrange("(n p) d -> p n d", p=P)

        def cols(w, a, n):
            return w[:, 0, a:a + n], w[:, 1, a:a + n]

        H = 2048
        WG0, WA0, WS0 = 0, E8 + E32, E8 + E32 + 4 * P
        JOBS = [
            [(cols(wgate, 0, E8), wg_d), (cols(wgate, E8, E32), gate_w_d),
             (cols(watt, 0, P), wq_d), (cols(watt, P, P), wk_d), (cols(watt, 2 * P, P), wv_d),
             (cols(watt, 3 * P, P), wo_d), (cols(wgu_g, PAIRS * P, P), sh_gate_d),
             (cols(wgu_u, PAIRS * P, P), sh_up_d), (cols(wdn, PAIRS * P, P), sh_down_d)],
            [(cols(w1, 0, H), w1_d[:, 0:H])], [(cols(w1, H, H), w1_d[:, H:2 * H])],
            [(cols(w2, 0, H), w2_d[:, 0:H])], [(cols(w2, H, H), w2_d[:, H:2 * H])],
            [(cols(wgu_g, 0, H), w_gate_d)], [(cols(wgu_u, 0, H), w_up_d)], [(cols(wdn, 0, H), w_down_d)],
        ]
        SMALL = [
            (b1T[:, :], b1_d), (b2row[:, :], b2_d), (bg_bc[:, :], bg_d.partition_broadcast(P)),
            (bq_col[:, :], bq_d), (bk_col[:, :], bk_d), (fb1_col[:, :], fb1_d),
            (gates[:, 0:2], g_xattn_d.partition_broadcast(P)), (gates[:, 2:4], g_ffn_d.partition_broadcast(P)),
        ] + [(gbias_bc[:, j, :], gate_bias_d.partition_broadcast(P)) for j in range(JT)] \
          + [(bv_bc[:, :], bv_d.partition_broadcast(P))] \
          + [(bo4[:, j, :], bo_d.partition_broadcast(P)) for j in range(JT)] \
          + [(fb2_4[:, j, :], fb2_d.partition_broadcast(P)) for j in range(JT)]
        N_CONST = 10
        GX0, GF0, GX1, GF1 = 0, 2, 1, 3

        def xt(c, j):
            return x_sb[:, bass.ds(c * JT + j, 1), :].rearrange("p a d -> p (a d)")

        def xchunk(c):
            return x_sb[:, bass.ds(c * JT, JT), :]

        LOOP = (3, NC - 1)

        def has(c):
            return not isinstance(c, int) or 0 <= c < NC

        def upto(c):
            return max(0, min(c, NC)) if isinstance(c, int) else c

        def run_pipeline(eng, body):
            for i in range(LOOP[0]):
                body(i)
            with eng.Fori(*LOOP) as i:
                body(i)
            for i in range(LOOP[1], NC + 2):
                body(i)

        def run_chunks(eng, body):
            body(0)
            with eng.Fori(1, NC) as i:
                body(i)

        nA.used, nB.used = (a_h_ready, E8 * FC), (b_gu_ready, NP)
        nC.used, nD.used = (c_qp_ready, 1), (d_h_ready, FC)
        cx["A"]["used"], cx["C"]["used"] = (a_logit_ready, 1), (c_vp_ready, 1)

        block = ctx.enter_context(nc.Block())

        @block.sync
        def _(sp):
            with nc.allow_non_contiguous_dma(reason="small columns and broadcasts, once"):
                for dst, src in SMALL:
                    sp.dma_start(dst, src).then_inc(small_loaded, 16)
            for n, job in enumerate(JOBS):
                if n >= 2:
                    sp.wait_ge(split_hi_done, n - 1)
                    sp.wait_ge(split_lo_done, n - 1)
                at = 0
                for (hi, _), src in job:
                    w = hi.shape[1]
                    sp.dma_start(stage[:, n % 2, at:at + w], src).then_inc(staged[n % 2], 16)
                    at += w
                if n == 0:
                    sp.dma_start(x_sb[:, :, :], x_dram).then_inc(x_loaded, 16)
            sp.dma_start(tern[:, 0, :], f1_d).then_inc(tern_loaded, 16)
            sp.dma_start(tern[:, 1, :], f2_d).then_inc(tern_loaded, 16)

            def load_ctx(s, c):
                at_least(sp, cx[s]["hi_ready"], c)
                at_least(sp, cx[s]["lo_ready"], c)
                sp.dma_start(cx[s]["f"][:, :], ctxT_d[:, bass.ds(c * CT, CT)]).then_inc(cx[s]["loaded"], 16)

            def store(c):
                sp.wait_ge(d_x_ready, c + 1)
                sp.dma_start(out_dram[:, bass.ds(c * JT, JT), :], x_out[:, :, :]).then_inc(stored, 16)

            run_chunks(sp, lambda c: load_ctx("A", c))
            load_ctx("C", 0)
            load_ctx("C", 1)
            with sp.Fori(2, NC) as i:
                load_ctx("C", i)
                store(i - 2)
            for c in (NC - 2, NC - 1):
                store(c)
            sp.wait_ge(stored, 16 * NC)

        @block.gpsimd
        def _(pool):
            steps = [0]

            def step(ins):
                ins.then_inc(pool_step, 1)
                steps[0] += 1
                pool.wait_ge(pool_step, steps[0])

            step(pool.memset(ident[:, :], 0.0))
            pool.affine_select(out=ident[:, :], in_=ident[:, :], compare_op=ALU.not_equal, fill=1.0, base=0,
                               pattern=[[-1, P]], channel_multiplier=1).then_inc(const_ready, 1)
            pool.memset(ones[:, :], 1.0).then_inc(const_ready, 1)
            pool.memset(ones16[:, :], 1.0).then_inc(const_ready, 1)
            pool.memset(unscale16[:, :], 1.0 / WSCALE).then_inc(const_ready, 1)
            pool.memset(half_pow[:, :], -0.5).then_inc(const_ready, 1)
            step(pool.memset(tri[:, :, :], 1.0))
            pool.affine_select(out=tri[:, :, :], in_=tri[:, :, :], compare_op=ALU.is_gt, fill=0.0, base=0,
                               pattern=[[1, 8], [-1, 8]], channel_multiplier=0).then_inc(const_ready, 1)
            v = hm[:, :, :]
            step(pool.memset(v, 1.0))
            step(pool.affine_select(out=v, in_=v, compare_op=ALU.is_ge, fill=0.0, base=0,
                                    pattern=[[-32, 4], [-8, 4]], channel_multiplier=1))
            step(pool.affine_select(out=v, in_=v, compare_op=ALU.is_ge, fill=0.0, base=7,
                                    pattern=[[32, 4], [8, 4]], channel_multiplier=-1))
            step(pool.tensor_tensor(hm[:, 0:2, :], hm[:, 0:2, :], hm[:, 2:4, :], ALU.add))
            pool.tensor_tensor(headmask[:, :], hm[:, 0, :], hm[:, 1, :], ALU.add).then_inc(const_ready, 1)
            step(pool.memset(sel[:, :, :, :], 0.0))
            step(pool.affine_select(out=sel[:, :, :, :], in_=sel[:, :, :, :], compare_op=ALU.not_equal,
                                    fill=1.0 / WSCALE, base=0, pattern=[[-2, PAIRS], [-1, 2], [0, SEQ]],
                                    channel_multiplier=1))
            pool.affine_select(out=sel[:, :, :, :], in_=sel[:, :, :, :], compare_op=ALU.not_equal,
                               fill=1.0 / WSCALE, base=-E32, pattern=[[-2, PAIRS], [-1, 2], [0, SEQ]],
                               channel_multiplier=1).then_inc(const_ready, 1)
            step(pool.memset(c_vbd[:, :, :, :, :], 0.0))
            pool.memset(c_vbd[0:SEQ, :, :, 0, DK:V9], 1.0).then_inc(const_ready, 1)
            pool.memset(c_vbd[SEQ:P, :, :, 1, DK:V9], 1.0).then_inc(const_ready, 1)

            def rstd(n, c):
                pool.wait_ge(n.var_ready, c + 1)
                pool.tensor_tensor(n.rstd[:, :], n.var_eps[:, :], half_pow[:, :], ALU.pow).then_inc(n.rstd_ready, 1)

            def low_part(c, e):
                pool.wait_ge(b_ah_ready, NP * c + e + 1)
                at_least(pool, b_down_done, NP * c + max(e - 2, 0))
                pool.tensor_tensor(b_al[:, e % 3, :], b_act[:, e % 2, :], b_ah[:, e % 3, :],
                                   ALU.subtract).then_inc(b_al_ready, 1)

            pool.wait_ge(const_ready, N_CONST)
            run_chunks(pool, lambda c: rstd(nA, c))
            rstd(nB, 0)

            def body(i):
                for e in range(NP):
                    if e == 0 and has(i - 1):
                        rstd(nC, i - 1)
                    if e == 9 and has(i - 2):
                        rstd(nD, i - 2)
                    if e == 15 and has(i + 1):
                        rstd(nB, i + 1)
                    if has(i):
                        low_part(i, e)

            run_pipeline(pool, body)

        @block.scalar
        def _(act):
            for n, job in enumerate(JOBS):
                act.wait_ge(staged[n % 2], 16 * sum(len(JOBS[m]) for m in range(n % 2, n + 1, 2)))
                at = 0
                for (hi, _), src in job:
                    w = hi.shape[1]
                    last = act.activation(hi, stage[:, n % 2, at:at + w], ACT.Copy, scale=WSCALE)
                    at += w
                last.then_inc(split_hi_done, 1)
            act.wait_ge(small_loaded, 16 * len(SMALL))
            act.activation(tg[:, :], gates[:, :], ACT.Tanh).then_inc(tanh_ready, 1)
            act.activation(b2s[:, 0, :], b2row[:, :], ACT.Copy, scale=WSCALE).then_inc(tanh_ready, 1)
            act.activation(bqs_col[:, :], bq_col[:, :], ACT.Copy, scale=DK ** -0.5).then_inc(tanh_ready, 1)
            act.wait_ge(tanh_ready, 3)

            def norm_hi(n, c):
                act.wait_ge(n.xT_ready, c + 1)
                at_least(act, n.used[0], n.used[1] * c)
                at_least(act, n.lo_ready, c)
                act.activation(n.hi[:, :], ps_misc[:, :], ACT.Copy).then_inc(n.hi_ready, 1)

            def ctx_hi(s, c):
                act.wait_ge(cx[s]["loaded"], 16 * (c + 1))
                at_least(act, cx[s]["used"][0], cx[s]["used"][1] * c)
                at_least(act, cx[s]["lo_ready"], c)
                act.activation(cx[s]["hi"][:, :], cx[s]["f"][:, :], ACT.Copy).then_inc(cx[s]["hi_ready"], 1)

            def a_chunk(c):
                ctx_hi("A", c)
                norm_hi(nA, c)
                act.wait_ge(a_shift_ready, c + 1)
                act.activation(a_exp[:, :, :], a_exp[:, :, :], ACT.Exp).then_inc(a_exp_ready, 1)
                for e in range(E8):
                    for k in range(FC):
                        n = E8 * FC * c + FC * e + k
                        act.wait_ge(a_h_ready, n + 1)
                        at_least(act, a_lo_ready, n - 3)
                        if k == 0:
                            at_least(act, a_y_ready, E8 * c + e - 1)
                        bias = b1T[:, FC * e + k:FC * e + k + 1]
                        act.activation(a_r[:, k, :], ps4[:, k, :], ACT.Relu, bias=bias, scale=1.0 / WSCALE)
                        act.activation(a_hh[:, e % 2, k, :], ps4[:, k, :], ACT.Relu, bias=bias,
                                       scale=1.0 / WSCALE).then_inc(a_hi_ready, 1)

            act.wait_ge(split_lo_done, len(JOBS))
            run_chunks(act, a_chunk)
            act.wait_ge(a_y_ready, E8 * NC)

            def score(c):
                act.wait_ge(b_route_ready, c + 1)
                at_least(act, b_comb_ready, c)
                act.activation(b_th[:, :], ps_misc[:, 0:JT * E32], ACT.Tanh, scale=0.5 / WSCALE)\
                   .then_inc(b_score_ready, 1)

            def comb_hi(c):
                act.wait_ge(b_combT_ready, c + 1)
                at_least(act, b_gu_ready, NP * c)
                at_least(act, b_cl_ready, c)
                act.activation(b_cT[0:E32, :], ps_misc[0:E32, :], ACT.Copy, scale=ROUTED_SCALE)\
                   .then_inc(b_ch_ready, 1)

            def silu(c, e):
                act.wait_ge(b_g_ready, NP * c + e + 1)
                at_least(act, b_u_used, NP * c + max(e - 1, 0))
                act.activation(b_silu[:, e % 2, :], ps4[:, e % 2, :], ACT.Silu, scale=1.0 / WSCALE)\
                   .then_inc(b_silu_ready, 1)

            def act_hi(c, e):
                act.wait_ge(b_act_ready, NP * c + e + 1)
                at_least(act, b_down_done, NP * c + max(e - 2, 0))
                act.activation(b_ah[:, e % 3, :], b_act[:, e % 2, :], ACT.Copy).then_inc(b_ah_ready, 1)

            def b_copy(c):
                act.wait_ge(b_down_done, NP * (c + 1))
                at_least(act, b_y_ready, c)
                act.activation(b_yT[:, :], ps_out[:, :], ACT.Copy).then_inc(b_yT_ready, 1)

            def query(c):
                act.wait_ge(c_qp_ready, c + 1)
                at_least(act, c_ql_ready, c)
                at_least(act, c_s_ready, BP * c)
                scale = DK ** -0.5 / WSCALE
                act.activation(c_q[:, :], ps_misc[:, :], ACT.Identity, bias=bqs_col[:, 0:1], scale=scale)
                act.activation(c_qh[:, :], ps_misc[:, :], ACT.Identity, bias=bqs_col[:, 0:1], scale=scale)\
                   .then_inc(c_q_ready, 1)

            def key(c):
                act.wait_ge(c_kp_ready, c + 1)
                at_least(act, c_km_ready, c)
                act.activation(c_k[:, :], ps_misc[:, :], ACT.Identity, bias=bk_col[:, 0:1], scale=1.0 / WSCALE)
                act.activation(c_kh[:, :], ps_misc[:, :], ACT.Identity, bias=bk_col[:, 0:1],
                               scale=1.0 / WSCALE).then_inc(c_k_ready, 1)

            def exps(c, p):
                act.wait_ge(c_shift_ready, BP * c + p + 1)
                act.activation(c_p[:, p % 2, :], c_p[:, p % 2, :], ACT.Exp).then_inc(c_exp_ready, 1)

            def probs_copy(c, p):
                act.wait_ge(c_pT_ready, BP * c + p + 1)
                at_least(act, c_o_ready, BP * c + p - 1)
                act.activation(c_pT[:, p % 2, :, :], ps2[:, :, :].rearrange("p a (h t) -> p (a h) t", t=P),
                               ACT.Copy).then_inc(c_pT_copied, 1)

            def o_hi(c):
                act.wait_ge(c_oT_ready, c + 1)
                at_least(act, c_y_ready, c)
                at_least(act, c_ol_ready, c)
                act.activation(c_oh[:, :], ps_misc[:, :], ACT.Copy).then_inc(c_oh_ready, 1)

            def gelu(c, k):
                act.wait_ge(d_h_ready, FC * c + k + 1)
                at_least(act, d_gl_ready, FC * (c - 1) + k + 1)
                act.activation(d_g[:, k, :], ps4[:, k, :], ACT.Gelu, bias=fb1_col[:, k:k + 1])\
                   .then_inc(d_g_ready, 1)

            norm_hi(nB, 0)
            score(0)
            comb_hi(0)

            def body(i):
                B, C, D = i, i - 1, i - 2
                for e in range(NP):
                    if has(B):
                        silu(B, e)
                        if e >= 1:
                            act_hi(B, e - 1)
                    if has(C):
                        if e == 1:
                            ctx_hi("C", C)
                        if e == 4:
                            norm_hi(nC, C)
                        if e == 6:
                            query(C)
                        if e == 8:
                            key(C)
                    if e == 14 and has(D):
                        norm_hi(nD, D)
                if has(B):
                    act_hi(B, NP - 1)
                    b_copy(B)
                if has(C):
                    exps(C, 0)
                if has(B + 1):
                    norm_hi(nB, B + 1)
                if has(C):
                    exps(C, 1)
                    probs_copy(C, 0)
                if has(B + 1):
                    score(B + 1)
                if has(C):
                    exps(C, 2)
                    probs_copy(C, 1)
                    exps(C, 3)
                    probs_copy(C, 2)
                    probs_copy(C, 3)
                    o_hi(C)
                if has(B + 1):
                    comb_hi(B + 1)
                if has(D):
                    for k in range(FC):
                        gelu(D, k)

            run_pipeline(act, body)

        @block.vector
        def _(dve):
            chain = Chain(dve, dve_chain)
            TT, TS, STT = dve.tensor_tensor, dve.tensor_scalar, dve.scalar_tensor_tensor

            def split_lo(n):
                dve.wait_ge(split_hi_done, n + 1)
                at = 0
                for (hi, lo), src in JOBS[n]:
                    w = hi.shape[1]
                    last = STT(out=lo, in0=stage[:, n % 2, at:at + w], scalar=WSCALE, in1=hi, op0=ALU.mult,
                               op1=ALU.subtract)
                    at += w
                last.then_inc(split_lo_done, 1)

            for n in range(len(JOBS)):
                split_lo(n)
            dve.wait_ge(tanh_ready, 3)
            STT(out=b2s[:, 1, :], in0=b2row[:, :], scalar=WSCALE, in1=b2s[:, 0, :], op0=ALU.mult,
                op1=ALU.subtract).then_inc(split_lo_done, 1)
            TS(tgs[:, :], tg[:, :], 1.0 / WSCALE, None, ALU.mult).then_inc(tgs_ready, 1)
            dve.wait_ge(tern_loaded, 32)
            dve.tensor_reduce(tern_sum[:, :], tern[:, :, :], AX.X, ALU.add, apply_absolute_value=True)\
               .then_inc(tern_abs_ready, 1)
            dve.wait_ge(tern_total_ready, 1)
            chain(TS(tern_hs[:, :], ps_out[:, 0:2], 1.0 / (P * FC * P), 1e-8, ALU.mult, ALU.max))
            chain.sync()
            chain(TS(tern_nhs[:, :], tern_hs[:, :], -0.5, None, ALU.mult))
            chain.sync()
            chain(TS(tern_hs[:, :], tern_nhs[:, :], -1.0, None, ALU.mult))
            chain.sync()
            for k in range(2):
                chain(TS(tern_neg[:, k, :], tern[:, k, :], tern_nhs[:, k:k + 1], None, ALU.is_lt))
            chain.sync()
            for k, w in enumerate((wt1, wt2)):
                STT(out=w[:, :], in0=tern[:, k, :], scalar=tern_hs[:, k:k + 1], in1=tern_neg[:, k, :],
                    op0=ALU.is_gt, op1=ALU.subtract).then_inc(tern_ready, 1)

            def norm(n, c):
                for j in range(JT):
                    chain(dve.bn_stats(n.stats[:, j, :], xt(c, j)))
                chain.sync()
                for j in range(JT):
                    chain(dve.bn_aggr(n.mean_var[:, j, :], n.stats[:, j, :]))
                chain.sync()
                TS(n.var_eps[:, :].unsqueeze(2), n.mean_var[:, :, 1:2], EPS, None, ALU.add)\
                    .then_inc(n.var_ready, 1)
                dve.wait_ge(n.rstd_ready, c + 1)
                at_least(dve, n.xT_ready, c)
                for j in range(JT):
                    last = TS(n.xn[:, j, :], xt(c, j), n.mean_var[:, j, 0:1], n.rstd[:, j:j + 1],
                              ALU.subtract, ALU.mult)
                last.then_inc(n.xn_ready, 1)

            def norm_lo(n, c):
                dve.wait_ge(n.hi_ready, c + 1)
                at_least(dve, n.used[0], n.used[1] * c)
                TT(n.lo[:, :], ps_misc[:, :], n.hi[:, :], ALU.subtract).then_inc(n.lo_ready, 1)

            def ctx_lo(s, c):
                dve.wait_ge(cx[s]["hi_ready"], c + 1)
                at_least(dve, cx[s]["used"][0], cx[s]["used"][1] * c)
                TT(cx[s]["lo"][:, :], cx[s]["f"][:, :], cx[s]["hi"][:, :], ALU.subtract)\
                    .then_inc(cx[s]["lo_ready"], 1)

            def rank8(s):
                shape = [P, JT, 8, 8]
                other, own = s.unsqueeze(2).to_broadcast(shape), s.unsqueeze(3).to_broadcast(shape)
                chain(TT(rk_gt[:, :, :, :], other, own, ALU.is_gt))
                chain(TT(rk_eq[:, :, :, :], other, own, ALU.is_equal))
                chain.sync()
                chain(TT(rk_eq[:, :, :, :], rk_eq[:, :, :, :], tri[:, :, :].unsqueeze(1).to_broadcast(shape),
                         ALU.mult))
                chain.sync()
                chain(TT(rk_gt[:, :, :, :], rk_gt[:, :, :, :], rk_eq[:, :, :, :], ALU.add))
                chain.sync()
                chain(dve.tensor_reduce(rk[:, :, :], rk_gt[:, :, :, :], AX.X, ALU.add))
                chain.sync()

            def a_route(c):
                shape = [P, JT, E8]
                dve.wait_ge(a_logit_ready, c + 1)
                chain(STT(out=a_logits[:, :, :], in0=ps_out[:, 0:JT * E8].rearrange("p (j e) -> p j e", e=E8),
                          scalar=1.0 / WSCALE, in1=bg_bc[:, :].unsqueeze(1).to_broadcast(shape),
                          op0=ALU.mult, op1=ALU.add))
                chain.sync()
                rank8(a_logits[:, :, :])
                chain(dve.tensor_reduce(a_max[:, :], a_logits[:, :, :], AX.X, ALU.max))
                chain.sync()
                TT(a_exp[:, :, :], a_logits[:, :, :], a_max[:, :].unsqueeze(2).to_broadcast(shape), ALU.subtract)\
                    .then_inc(a_shift_ready, 1)
                dve.wait_ge(a_exp_ready, c + 1)
                chain(STT(out=a_w[:, :, :], in0=rk[:, :, :], scalar=1.5, in1=a_exp[:, :, :], op0=ALU.is_lt,
                          op1=ALU.mult))
                chain.sync()
                chain(dve.tensor_reduce(a_sum[:, :], a_w[:, :, :], AX.X, ALU.add))
                chain.sync()
                chain(dve.reciprocal(a_rec[:, :], a_sum[:, :]))
                chain.sync()
                chain(TT(a_w[:, :, :], a_w[:, :, :], a_rec[:, :].unsqueeze(2).to_broadcast(shape), ALU.mult))
                chain.sync()

            def a_lo(c, e):
                for k in range(FC):
                    n = E8 * FC * c + FC * e + k
                    dve.wait_ge(a_hi_ready, n + 1)
                    if k == 0:
                        at_least(dve, a_y_ready, E8 * c + e - 1)
                    TT(a_hl[:, e % 2, k, :], a_r[:, k, :], a_hh[:, e % 2, k, :], ALU.subtract)\
                        .then_inc(a_lo_ready, 1)

            def a_add(c, e):
                dve.wait_ge(a_y_ready, E8 * c + e + 1)
                if e >= 1:
                    dve.wait_ge(a_y_used, E8 * c + e)
                for j in range(JT):
                    y, w, acc = ps2[:, e % 2, j * P:(j + 1) * P], a_w[:, j, e:e + 1], a_acc[:, j, :]
                    if e == 0:
                        last = TS(acc, y, w, None, ALU.mult)
                    else:
                        last = STT(out=acc, in0=y, scalar=w, in1=acc, op0=ALU.mult, op1=ALU.add)
                last.then_inc(a_y_used, 1)

            def a_chunk(c):
                chain.restart()
                norm(nA, c)
                ctx_lo("A", c)
                norm_lo(nA, c)
                a_route(c)
                for e in range(E8):
                    a_lo(c, e)
                    if e >= 1:
                        a_add(c, e - 1)
                a_add(c, E8 - 1)
                dve.wait_ge(a_y_used, E8 * (c + 1))
                STT(out=xchunk(c), in0=a_acc[:, :, :], scalar=tgs[:, GX0:GX0 + 1], in1=xchunk(c),
                    op0=ALU.mult, op1=ALU.add).then_inc(a_x_done, 1)

            dve.wait_ge(x_loaded, 16)
            dve.wait_ge(tgs_ready, 1)
            dve.wait_ge(const_ready, N_CONST)
            dve.wait_ge(small_loaded, 16 * len(SMALL))
            for odd, rows in ((0, slice(0, SEQ)), (1, slice(SEQ, P))):
                src = bv_bc[rows, :].rearrange("p (n o k) -> p n o k", o=2, k=DK)[:, :, odd, :]
                chain(dve.tensor_copy(bv8[rows, :].rearrange("p (b n k) -> p b n k", b=NB, k=DK),
                                      src.unsqueeze(1).to_broadcast([SEQ, NB, HEADS // 2, DK])))
            run_chunks(dve, a_chunk)
            dve.wait_ge(a_x_done, NC)
            dve.wait_ge(a_y_ready, E8 * NC)

            G4 = JT * GROUPS

            def route_groups(c):
                dve.wait_ge(b_score_ready, c + 1)
                chain(TS(b_sc[:, :, :], b_th[:, :].rearrange("p (j e) -> p j e", e=E32), 0.5, 0.5,
                         ALU.mult, ALU.add))
                chain.sync()
                chain(TT(b_scb[:, :, :, :].rearrange("p (j g) a b -> p j (g a b)", j=JT), b_sc[:, :, :],
                         gbias_bc[:, :, :], ALU.add))
                chain.sync()
                a, b = b_scb[:, :, :, 0], b_scb[:, :, :, 1]
                chain(TT(b_mx[:, :, :], a, b, ALU.max))
                chain(TT(b_mn[:, :, :], a, b, ALU.min))
                chain.sync()
                chain(TT(b_t1[:, :], b_mx[:, :, 0], b_mx[:, :, 1], ALU.max))
                chain(TT(b_t2[:, :], b_mx[:, :, 0], b_mx[:, :, 1], ALU.min))
                chain(TT(b_t3[:, :], b_mn[:, :, 0], b_mn[:, :, 1], ALU.max))
                chain.sync()
                chain(TT(b_t2[:, :], b_t2[:, :], b_t3[:, :], ALU.max))
                chain.sync()
                chain(TT(b_gs[:, :, :].rearrange("p j g -> p (j g)"), b_t1[:, :], b_t2[:, :], ALU.add))
                chain.sync()

            def route_mask(c):
                rank8(b_gs[:, :, :])
                chain(TS(b_gm[:, :, :], rk[:, :, :], TOP_GROUPS - 0.5, None, ALU.is_lt))
                chain.sync()
                scb = b_scb[:, :, :, :].rearrange("p g a b -> p g (a b)")
                chain(TT(b_masked[:, :, :].rearrange("p j (g k) -> p (j g) k", k=PER_GROUP), scb,
                         b_gm[:, :, :].rearrange("p j g -> p (j g)").unsqueeze(2).to_broadcast([P, G4, PER_GROUP]),
                         ALU.mult))
                chain.sync()

            def route_top(c):
                for j in range(JT):
                    chain(dve.max(b_m8[:, j, :], b_masked[:, j, :]))
                chain.sync()
                for j in range(JT):
                    chain(dve.match_replace(b_mr[:, j, :], b_m8[:, j, :], b_masked[:, j, :], -3e38))
                chain.sync()
                chain(STT(out=b_ws[:, :, :], in0=b_mr[:, :, :], scalar=-1e38, in1=b_sc[:, :, :], op0=ALU.is_lt,
                          op1=ALU.mult))
                chain.sync()
                chain(dve.tensor_reduce(b_wsum[:, :], b_ws[:, :, :], AX.X, ALU.add))
                chain.sync()
                chain(TS(b_wsum[:, :], b_wsum[:, :], 1e-20, None, ALU.add))
                chain.sync()
                chain(dve.reciprocal(b_wrec[:, :], b_wsum[:, :]))
                chain.sync()
                at_least(dve, b_combT_ready, c)
                TT(b_comb[:, :, :], b_ws[:, :, :], b_wrec[:, :].unsqueeze(2).to_broadcast([P, JT, E32]), ALU.mult)\
                    .then_inc(b_comb_ready, 1)

            def comb_lo(c):
                dve.wait_ge(b_ch_ready, c + 1)
                at_least(dve, b_gu_ready, NP * c)
                STT(out=b_cT[E32:2 * E32, :], in0=ps_misc[0:E32, :], scalar=ROUTED_SCALE, in1=b_cT[0:E32, :],
                    op0=ALU.mult, op1=ALU.subtract).then_inc(b_cl_ready, 1)

            def pair(c, e):
                n = NP * c + e
                dve.wait_ge(b_silu_ready, n + 1)
                dve.wait_ge(b_gu_ready, n + 1)
                TT(b_su[:, e % 2, :], ps4[:, 2 + e % 2, :], b_silu[:, e % 2, :], ALU.mult).then_inc(b_u_used, 1)
                dve.wait_ge(b_u_used, n + 1)
                at_least(dve, b_al_ready, NP * c + max(e - 1, 0))
                TT(b_act[:, e % 2, :], ps2[:, e % 2, :], b_su[:, e % 2, :], ALU.mult).then_inc(b_act_ready, 1)

            def b_update(c):
                dve.wait_ge(b_y_ready, c + 1)
                STT(out=xchunk(c), in0=ps_misc[:, :].rearrange("p (j d) -> p j d", d=P),
                    scalar=tgs[:, GF0:GF0 + 1], in1=xchunk(c), op0=ALU.mult, op1=ALU.add).then_inc(b_x_done, 1)

            def query_lo(c):
                dve.wait_ge(c_q_ready, c + 1)
                at_least(dve, c_s_ready, BP * c)
                TT(c_ql[:, :], c_q[:, :], c_qh[:, :], ALU.subtract).then_inc(c_ql_ready, 1)

            def key_masks(c):
                dve.wait_ge(c_k_ready, c + 1)
                at_least(dve, c_s_ready, BP * c)
                chain(TT(c_kl[:, :], c_k[:, :], c_kh[:, :], ALU.subtract))
                for r in range(4):
                    chain(TS(c_km[:, 0, r, :], c_kh[:, :], headmask[:, r:r + 1], None, ALU.mult))
                chain.sync()
                for r in range(4):
                    last = TS(c_km[:, 1, r, :], c_kl[:, :], headmask[:, r:r + 1], None, ALU.mult)
                last.then_inc(c_km_ready, 1)

            def values(c):
                dve.wait_ge(c_vp_ready, c + 1)
                at_least(dve, c_o_ready, BP * c)
                for odd, rows in ((0, slice(0, SEQ)), (1, slice(SEQ, P))):
                    out = c_vbd[rows, :, :, odd, 0:DK].rearrange("p b n k -> p (b n) k")
                    last = STT(out=out, in0=ps_misc[rows, :].rearrange("p (n k) -> p n k", k=DK),
                               scalar=1.0 / WSCALE, in1=bv8[rows, :].rearrange("p (n k) -> p n k", k=DK),
                               op0=ALU.mult, op1=ALU.add)
                last.then_inc(c_v_ready, 1)

            def shift(c, p):
                s = ps4[:, :, 0:4 * SEQ].rearrange("p q (r s) -> p q r s", s=SEQ)
                dve.wait_ge(c_s_ready, BP * c + p + 1)
                m = c_max[:, :].rearrange("p (q r) -> p q r", r=4)
                chain(dve.tensor_reduce(m, s, AX.X, ALU.max))
                chain.sync()
                at_least(dve, c_pT_ready, BP * c + p - 1)
                TT(c_p[:, p % 2, :].rearrange("p (q r s) -> p q r s", q=4, r=4), s,
                   m.unsqueeze(3).to_broadcast([P, 4, 4, SEQ]), ALU.subtract).then_inc(c_shift_ready, 1)

            def heads_norm(c, p):
                dve.wait_ge(c_o_ready, BP * c + p + 1)
                o = ps_out[:, 0:HEADS * V9].rearrange("p (h k) -> p h k", k=V9)
                chain(dve.reciprocal(c_rec[:, :].unsqueeze(2), o[:, :, DK:V9]))
                chain.sync()
                if p == 0:
                    at_least(dve, c_oT_ready, c)
                TT(c_on[:, p, :, :], o[:, :, 0:DK], c_rec[:, :].unsqueeze(2).to_broadcast([P, HEADS, DK]),
                   ALU.mult).then_inc(c_on_ready, 1)

            def o_lo(c):
                dve.wait_ge(c_oh_ready, c + 1)
                at_least(dve, c_y_ready, c)
                TT(c_ol[:, :], ps_misc[:, :], c_oh[:, :], ALU.subtract).then_inc(c_ol_ready, 1)

            def c_update(c):
                dve.wait_ge(c_y_ready, c + 1)
                STT(out=c_y[:, :, :], in0=ps_out[:, :].rearrange("p (j d) -> p j d", d=P), scalar=1.0 / WSCALE,
                    in1=bo4[:, :, :], op0=ALU.mult, op1=ALU.add).then_inc(c_y_used, 1)
                dve.wait_ge(c_y_used, c + 1)
                STT(out=xchunk(c), in0=c_y[:, :, :], scalar=tg[:, GX1:GX1 + 1], in1=xchunk(c), op0=ALU.mult,
                    op1=ALU.add).then_inc(c_x_done, 1)

            def gelu_split(c, k):
                dve.wait_ge(d_g_ready, FC * c + k + 1)
                if k == 0:
                    at_least(dve, d_y_ready, c)
                chain(dve.tensor_copy(d_gh[:, k, :], d_g[:, k, :]))
                chain.sync()
                TT(d_gl[:, k, :], d_g[:, k, :], d_gh[:, k, :], ALU.subtract).then_inc(d_gl_ready, 1)

            def d_update(c):
                dve.wait_ge(d_y_ready, c + 1)
                chain(TT(d_y[:, :, :], ps_out[:, :].rearrange("p (j d) -> p j d", d=P), fb2_4[:, :, :], ALU.add))
                chain.sync()
                at_least(dve, stored, 16 * c)
                STT(out=x_out[:, :, :], in0=d_y[:, :, :], scalar=tg[:, GF1:GF1 + 1], in1=xchunk(c), op0=ALU.mult,
                    op1=ALU.add).then_inc(d_x_ready, 1)

            chain.restart()
            norm(nB, 0)
            norm_lo(nB, 0)
            route_groups(0)
            route_mask(0)
            route_top(0)
            comb_lo(0)

            def body(i):
                B, C, D = i, i - 1, i - 2
                chain.restart()
                for e in range(NP):
                    if has(C):
                        if e == 0:
                            dve.wait_ge(b_x_done, C + 1)
                            norm(nC, C)
                        if e == 2:
                            ctx_lo("C", C)
                        if e == 4:
                            norm_lo(nC, C)
                        if e == 6:
                            query_lo(C)
                        if e == 8:
                            key_masks(C)
                        if e == 11:
                            values(C)
                    if has(D):
                        if e == 9:
                            dve.wait_ge(c_x_done, D + 1)
                            norm(nD, D)
                        if e == 14:
                            norm_lo(nD, D)
                    if e == 15 and has(B + 1):
                        norm(nB, B + 1)
                    if has(B):
                        pair(B, e)
                if has(B):
                    b_update(B)
                if has(C):
                    shift(C, 0)
                if has(B + 1):
                    norm_lo(nB, B + 1)
                if has(C):
                    shift(C, 1)
                if has(B + 1):
                    route_groups(B + 1)
                if has(C):
                    shift(C, 2)
                    heads_norm(C, 0)
                if has(B + 1):
                    route_mask(B + 1)
                if has(C):
                    shift(C, 3)
                    heads_norm(C, 1)
                if has(B + 1):
                    route_top(B + 1)
                if has(C):
                    heads_norm(C, 2)
                    heads_norm(C, 3)
                    o_lo(C)
                if has(B + 1):
                    comb_lo(B + 1)
                if has(C):
                    c_update(C)
                if has(D):
                    for k in range(FC):
                        gelu_split(D, k)
                    d_update(D)

            run_pipeline(dve, body)

        @block.tensor
        def _(pe):
            def split_mm(out, w, x, start=True, stop=True):
                pe.matmul(out, w[0], x[0], start=start, stop=False)
                pe.matmul(out, w[0], x[1], start=False, stop=False)
                return pe.matmul(out, w[1], x[0], start=False, stop=stop)

            def wpart(w, k):
                return w[:, 0, k * P:(k + 1) * P], w[:, 1, k * P:(k + 1) * P]

            def transpose4(out, src):
                for j in range(JT):
                    last = pe.transpose(out[:, j * P:(j + 1) * P], src[:, j, :], ident[:, :])
                return last

            misc = []

            def misc_use(sem_, count):
                if misc:
                    pe.wait_ge(*misc.pop())
                misc.append((sem_, count))

            def norm_T(n, c):
                misc_use(n.lo_ready, c + 1)
                pe.wait_ge(n.xn_ready, c + 1)
                transpose4(ps_misc, n.xn).then_inc(n.xT_ready, 1)

            pe.wait_ge(const_ready, N_CONST)
            pe.wait_ge(tern_abs_ready, 1)
            pe.matmul(ps_out[:, 0:2], ones[:, :], tern_sum[:, :], start=True, stop=True)\
              .then_inc(tern_total_ready, 1)
            pe.wait_ge(tern_ready, 2)
            pe.wait_ge(split_hi_done, len(JOBS))
            pe.wait_ge(split_lo_done, len(JOBS) + 1)

            def a_hidden(c, e):
                for k in range(FC):
                    n = E8 * FC * c + FC * e + k
                    at_least(pe, a_hi_ready, n - FC + 1)
                    split_mm(ps4[:, k, :], wpart(w1, FC * e + k), (nA.hi[:, :], nA.lo[:, :]))\
                        .then_inc(a_h_ready, 1)

            def a_out(c, e):
                pe.wait_ge(a_lo_ready, FC * (E8 * c + e + 1))
                at_least(pe, a_y_used, E8 * c + e - 1)
                for j in range(JT):
                    out, t = ps2[:, e % 2, j * P:(j + 1) * P], slice(j * P, (j + 1) * P)
                    for k in range(FC):
                        h = (a_hh[:, e % 2, k, t], a_hl[:, e % 2, k, t])
                        split_mm(out, h, wpart(w2, FC * e + k), start=(k == 0), stop=False)
                    for part in range(2):
                        last = pe.matmul(out, ones16[:, 0:P], b2s[:, part, e * P:(e + 1) * P], start=False,
                                         stop=(part == 1))
                last.then_inc(a_y_ready, 1)

            def a_chunk(c):
                norm_T(nA, c)
                pe.wait_ge(cx["A"]["hi_ready"], c + 1)
                pe.wait_ge(cx["A"]["lo_ready"], c + 1)
                at_least(pe, a_y_used, E8 * c)
                for j in range(JT):
                    t = slice(j * P, (j + 1) * P)
                    ch, cl = cx["A"]["hi"][:, t], cx["A"]["lo"][:, t]
                    out = ps_out[:, j * E8:(j + 1) * E8]
                    split_mm(out, (ch, cl), (wgate[:, 0, 0:E8], wgate[:, 1, 0:E8]), stop=False)
                    last = pe.matmul(out, cl, wgate[:, 1, 0:E8], start=False, stop=True)
                last.then_inc(a_logit_ready, 1)
                pe.wait_ge(nA.hi_ready, c + 1)
                pe.wait_ge(nA.lo_ready, c + 1)
                a_hidden(c, 0)
                for e in range(1, E8):
                    a_hidden(c, e)
                    a_out(c, e - 1)
                a_out(c, E8 - 1)

            a_chunk(0)
            with pe.Fori(1, NC) as i:
                misc[:] = [(nA.lo_ready, i)]
                a_chunk(i)
            misc[:] = [(nA.lo_ready, NC)]

            def route(c):
                misc_use(b_score_ready, c + 1)
                pe.wait_ge(nB.hi_ready, c + 1)
                pe.wait_ge(nB.lo_ready, c + 1)
                for j in range(JT):
                    t = slice(j * P, (j + 1) * P)
                    out = ps_misc[:, j * E32:(j + 1) * E32]
                    g = wgate[:, 0, E8:E8 + E32], wgate[:, 1, E8:E8 + E32]
                    split_mm(out, (nB.hi[:, t], nB.lo[:, t]), g, stop=False)
                    last = pe.matmul(out, nB.lo[:, t], g[1], start=False, stop=True)
                last.then_inc(b_route_ready, 1)

            def comb_T(c):
                misc_use(b_cl_ready, c + 1)
                pe.wait_ge(b_comb_ready, c + 1)
                for j in range(JT):
                    last = pe.transpose(ps_misc[0:E32, j * P:(j + 1) * P], b_comb[:, j, :], ident[:, :])
                last.then_inc(b_combT_ready, 1)

            def gate_up(c, e):
                x = (nB.hi[:, :], nB.lo[:, :])
                if e == 0:
                    pe.wait_ge(b_cl_ready, c + 1)
                    at_least(pe, c_shift_ready, BP * upto(c - 1))
                    at_least(pe, d_g_ready, FC * upto(c - 2))
                    at_least(pe, c_pT_copied, BP * upto(c - 1))
                at_least(pe, b_u_used, NP * c + max(e - 1, 0))
                split_mm(ps4[:, e % 2, :], wpart(wgu_g, e), x).then_inc(b_g_ready, 1)
                split_mm(ps4[:, 2 + e % 2, :], wpart(wgu_u, e), x)
                at_least(pe, b_act_ready, NP * c + max(e - 1, 0))
                if e < PAIRS:
                    w = sel[:, e, :, :].rearrange("p a b -> p (a b)")
                    last = pe.matmul(ps2[:, e % 2, :], w, b_cT[:, :], start=True, stop=True)
                else:
                    last = pe.matmul(ps2[:, e % 2, :], unscale16[:, :], ones16[:, :], start=True, stop=True)
                last.then_inc(b_gu_ready, 1)

            def down(c, e):
                if e == 0:
                    at_least(pe, c_y_used, upto(c - 1))
                    at_least(pe, d_x_ready, upto(c - 2))
                    at_least(pe, b_yT_ready, upto(c))
                pe.wait_ge(b_ah_ready, NP * c + e + 1)
                pe.wait_ge(b_al_ready, NP * c + e + 1)
                split_mm(ps_out[:, :], wpart(wdn, e), (b_ah[:, e % 3, :], b_al[:, e % 3, :]),
                         start=(e == 0), stop=(e == NP - 1)).then_inc(b_down_done, 1)

            def b_out_T(c):
                misc_use(b_x_done, c + 1)
                pe.wait_ge(b_yT_ready, c + 1)
                for j in range(JT):
                    t = slice(j * P, (j + 1) * P)
                    last = pe.transpose(ps_misc[:, t], b_yT[:, t], ident[:, :])
                last.then_inc(b_y_ready, 1)

            def query(c):
                misc_use(c_q_ready, c + 1)
                pe.wait_ge(nC.hi_ready, c + 1)
                split_mm(ps_misc[:, :], wpart(watt, 0), (nC.hi[:, :], nC.lo[:, :])).then_inc(c_qp_ready, 1)

            def key(c):
                misc_use(c_k_ready, c + 1)
                pe.wait_ge(cx["C"]["hi_ready"], c + 1)
                pe.wait_ge(cx["C"]["lo_ready"], c + 1)
                split_mm(ps_misc[:, :], wpart(watt, 1), (cx["C"]["hi"][:, :], cx["C"]["lo"][:, :]))\
                    .then_inc(c_kp_ready, 1)

            def values(c):
                misc_use(c_v_ready, c + 1)
                for b in range(NB):
                    t = slice(b * SEQ, (b + 1) * SEQ)
                    for odd in range(2):
                        out = ps_misc[odd * SEQ:odd * SEQ + SEQ, b * SEQ:(b + 1) * SEQ]
                        w = [watt[:, part, 2 * P:3 * P].rearrange("p (n o k) -> p n o k", o=2, k=DK)[:, :, odd, :]
                             for part in range(2)]
                        last = split_mm(out, (cx["C"]["hi"][:, t], cx["C"]["lo"][:, t]), w)
                last.then_inc(c_vp_ready, 1)

            def scores(c, i, p):
                if p == 0:
                    for s in (c_q_ready, c_ql_ready, c_km_ready):
                        pe.wait_ge(s, c + 1)
                    at_least(pe, b_u_used, NP * upto(i + 1))
                    at_least(pe, d_g_ready, FC * upto(i - 2))
                at_least(pe, c_shift_ready, BP * c + p)
                for half in range(2):
                    t = slice((2 * p + half) * SEQ, (2 * p + half + 1) * SEQ)
                    for q in range(4):
                        rows = slice(32 * q, 32 * q + 32)
                        out = ps4[half * SEQ:half * SEQ + SEQ, q, 0:4 * SEQ]
                        last = split_mm(out, (c_qh[rows, t], c_ql[rows, t]),
                                        (c_km[rows, 0, :, t], c_km[rows, 1, :, t]))
                last.then_inc(c_s_ready, 1)

            def probs_T(c, i, p):
                pe.wait_ge(c_exp_ready, BP * c + p + 1)
                if p == 0:
                    at_least(pe, b_act_ready, NP * upto(i + 1))
                at_least(pe, c_pT_copied, BP * c + p)
                for h in range(HEADS // 2):
                    last = pe.transpose(ps2[:, h // 4, (h % 4) * P:(h % 4 + 1) * P],
                                        c_p[:, p % 2, h * P:(h + 1) * P], ident[:, :])
                last.then_inc(c_pT_ready, 1)

            def weighted(c, i, p):
                pe.wait_ge(c_pT_copied, BP * c + p + 1)
                if p == 0:
                    pe.wait_ge(c_v_ready, c + 1)
                    at_least(pe, b_yT_ready, upto(i + 1))
                    at_least(pe, d_x_ready, upto(i - 2))
                at_least(pe, c_on_ready, BP * c + p)
                for half in range(2):
                    for h in range(HEADS // 2):
                        o = h * 2 * V9
                        last = pe.matmul(ps_out[half * SEQ:half * SEQ + SEQ, o:o + 2 * V9],
                                         c_pT[:, p % 2, h, half * SEQ:half * SEQ + SEQ],
                                         c_vbd[:, 2 * p + half, h, :, :].rearrange("p a b -> p (a b)"),
                                         start=True, stop=True)
                last.then_inc(c_o_ready, 1)

            def o_T(c):
                misc_use(c_ol_ready, c + 1)
                pe.wait_ge(c_on_ready, BP * (c + 1))
                for j in range(JT):
                    last = pe.transpose(ps_misc[:, j * P:(j + 1) * P],
                                        c_on[:, j, :, :].rearrange("p h k -> p (h k)"), ident[:, :])
                last.then_inc(c_oT_ready, 1)

            def project(c):
                pe.wait_ge(c_oh_ready, c + 1)
                pe.wait_ge(c_ol_ready, c + 1)
                for j in range(JT):
                    t = slice(j * P, (j + 1) * P)
                    last = split_mm(ps_out[:, t], (c_oh[:, t], c_ol[:, t]), wpart(watt, 3))
                last.then_inc(c_y_ready, 1)

            def d_hidden(c, i):
                pe.wait_ge(nD.hi_ready, c + 1)
                pe.wait_ge(nD.lo_ready, c + 1)
                at_least(pe, c_shift_ready, BP * upto(i))
                at_least(pe, d_g_ready, FC * c)
                for k in range(FC):
                    w = wt1[:, k * P:(k + 1) * P]
                    pe.matmul(ps4[:, k, :], w, nD.hi[:, :], start=True, stop=False)
                    pe.matmul(ps4[:, k, :], w, nD.lo[:, :], start=False, stop=True).then_inc(d_h_ready, 1)

            def d_out(c, i):
                pe.wait_ge(d_gl_ready, FC * (c + 1))
                at_least(pe, c_y_used, upto(i))
                at_least(pe, d_x_ready, c)
                for j in range(JT):
                    t = slice(j * P, (j + 1) * P)
                    for k in range(FC):
                        w = wt2[:, k * P:(k + 1) * P]
                        pe.matmul(ps_out[:, t], d_gh[:, k, t], w, start=(k == 0), stop=False)
                        last = pe.matmul(ps_out[:, t], d_gl[:, k, t], w, start=False, stop=(k == FC - 1))
                last.then_inc(d_y_ready, 1)

            norm_T(nB, 0)
            route(0)
            comb_T(0)

            def body(i):
                B, C, D = i, i - 1, i - 2
                if not isinstance(i, int):
                    misc[:] = [(b_cl_ready, i + 1)]
                for e in range(NP):
                    if has(C):
                        if e == 3:
                            norm_T(nC, C)
                        if e == 5:
                            query(C)
                        if e == 7:
                            key(C)
                        if e == 9:
                            values(C)
                    if e == 13 and has(D):
                        norm_T(nD, D)
                    if has(B):
                        gate_up(B, e)
                        if e >= 2:
                            down(B, e - 2)
                if has(B):
                    down(B, NP - 2)
                    down(B, NP - 1)
                    b_out_T(B)
                if has(C):
                    scores(C, i, 0)
                if has(B + 1):
                    norm_T(nB, B + 1)
                if has(C):
                    scores(C, i, 1)
                    probs_T(C, i, 0)
                if has(B + 1):
                    route(B + 1)
                if has(C):
                    scores(C, i, 2)
                    probs_T(C, i, 1)
                    weighted(C, i, 0)
                    scores(C, i, 3)
                    probs_T(C, i, 2)
                    weighted(C, i, 1)
                    probs_T(C, i, 3)
                    weighted(C, i, 2)
                    weighted(C, i, 3)
                    o_T(C)
                    project(C)
                if has(B + 1):
                    comb_T(B + 1)
                if has(D):
                    d_hidden(D, i)
                    d_out(D, i)

            for i in range(LOOP[0]):
                body(i)
            with pe.Fori(*LOOP) as i:
                body(i)
            misc[:] = [(b_cl_ready, LOOP[1] + 1)]
            for i in range(LOOP[1], NC + 2):
                body(i)


def kernel(**inputs):
    import numpy as np
    import concourse.bacc as bacc
    from concourse import mybir as mb
    from concourse.bass_utils import run_bass_kernel_spmd

    a = {k: np.asarray(v) for k, v in inputs.items()}
    T = a["x"].shape[0] * a["x"].shape[1]

    def row(v):
        return v.reshape(1, -1)

    def col(v):
        return v.reshape(-1, 1)

    def parts(v, n):
        return v.reshape(n, P, -1).transpose(1, 0, 2).reshape(P, -1)

    w1, w2 = a["L0_xattn_W1"], a["L0_xattn_W2"]
    arrays = {
        "x": a["x"].reshape(T, P),
        "ctxT": a["ctx_1024"].reshape(T, P).T,
        "g_xattn": a["g_xattn"], "g_ffn": a["g_ffn"],
        "a_wg": a["L0_xattn_Wg"], "a_bg": a["L0_xattn_bg"],
        "a_w1": w1.transpose(1, 0, 2).reshape(P, -1),
        "a_b1": a["L0_xattn_b1"].reshape(-1, P).T,
        "a_w2": parts(w2.reshape(-1, P), w2.shape[0] * w2.shape[1] // P),
        "a_b2": row(a["L0_xattn_b2"]),
        "b_gate_w": a["L0_ffn_gate_w"].T, "b_gate_bias": a["L0_ffn_gate_bias"],
        "b_w_gate": a["L0_ffn_w_gate"].reshape(-1, P).T,
        "b_w_up": a["L0_ffn_w_up"].reshape(-1, P).T,
        "b_w_down": parts(a["L0_ffn_w_down"].transpose(0, 2, 1).reshape(-1, P), 16),
        "b_sh_gate": a["L0_ffn_sh_gate"].T, "b_sh_up": a["L0_ffn_sh_up"].T, "b_sh_down": a["L0_ffn_sh_down"].T,
        "c_wq": a["L1_xattn_W_Q"], "c_bq": col(a["L1_xattn_b_Q"]),
        "c_wk": a["L1_xattn_W_K"], "c_bk": col(a["L1_xattn_b_K"]),
        "c_wv": a["L1_xattn_W_V"], "c_bv": a["L1_xattn_b_V"],
        "c_wo": a["L1_xattn_W_O"], "c_bo": a["L1_xattn_b_O"],
        "d_w1": a["L1_ffn_W1"].T, "d_b1": a["L1_ffn_b1"].reshape(-1, P).T,
        "d_w2": parts(a["L1_ffn_W2"].T, 4), "d_b2": a["L1_ffn_b2"],
    }
    arrays = {k: np.ascontiguousarray(v) for k, v in arrays.items()}
    nc = bacc.Bacc("TRN2", target_bir_lowering=False, num_devices=1)
    args = [nc.dram_tensor(k, v.shape, mb.dt.from_np(v.dtype), kind="ExternalInput").ap()
            for k, v in arrays.items()]
    args.append(nc.dram_tensor("out", (T, P), mb.dt.float32, kind="ExternalOutput").ap())
    build_flamingo(nc, *args)
    r = run_bass_kernel_spmd(nc, [arrays], core_ids=[0])
    return r.results[0]["out"].reshape(a["x"].shape)
```

```python
from contextlib import ExitStack

import concourse.bass as bass
from concourse import mybir

F32 = mybir.dt.float32
F16 = mybir.dt.float16
I32 = mybir.dt.int32
U32 = mybir.dt.uint32
ALU = mybir.AluOpType
ACT = mybir.ActivationFunctionType
AX = mybir.AxisListType

P = 128
CT = 512
JT = CT // P
WSCALE = 64.0
EPS = 1e-5
SEQ = 64
HEADS, DK = 16, 8
ROUTED_SCALE = 2.5
ROWS = 256
TOP = 2


class Chain:

    def __init__(self, eng, sem):
        self.eng, self.sem, self.n = eng, sem, 0

    def __call__(self, ins):
        ins.then_inc(self.sem, 1)
        self.n += 1
        return ins

    def sync(self):
        self.eng.wait_ge(self.sem, self.n)

    def restart(self):
        if self.n:
            self.sync()
        self.eng.sem_clear(self.sem)
        self.n = 0


def at_least(eng, sem, count):
    if isinstance(count, int) and count <= 0:
        return
    eng.wait_ge(sem, count)


class Norm:

    def __init__(self, name, sb, sem):
        self.stats = sb(name + "_stats", [P, JT, 6], F32)
        self.mean_var = sb(name + "_mean_var", [P, JT, 2], F32)
        self.var_eps = sb(name + "_var_eps", [P, JT], F32)
        self.rstd = sb(name + "_rstd", [P, JT], F32)
        self.neg_mean = sb(name + "_neg_mean", [P, JT], F32)
        self.offset = sb(name + "_offset", [P, JT], F32)
        self.xn = sb(name + "_xn", [P, JT, P], F32)
        self.hi = sb(name + "_hi", [P, CT], F16)
        self.lo = sb(name + "_lo", [P, CT], F16)
        self.var_ready = sem(name + "_var_ready")
        self.rstd_ready = sem(name + "_rstd_ready")
        self.offset_ready = sem(name + "_offset_ready")
        self.xn_ready = sem(name + "_xn_ready")
        self.xT_ready = sem(name + "_xT_ready")
        self.hi_ready = sem(name + "_hi_ready")
        self.lo_ready = sem(name + "_lo_ready")


def build_flamingo(nc, x_d, ctxT_d, g_xattn_d, g_ffn_d, wg_d, bg_d, w1_d, b1_d, w2_d, b2_d,
                   gate_w_d, gate_bias_d, w_gate_d, w_up_d, w_down_d, sh_gate_d, sh_up_d, sh_down_d,
                   wq_d, bq_d, wk_d, bk_d, wv_d, bv_d, wo_d, bo_d, f1_d, fb1_d, f2_d, fb2_d, out_d):
    T = x_d.shape[0]
    NT, NC = T // P, T // CT
    E8, FC = 8, 4
    E32, PAIRS = 32, 16
    NP = PAIRS + 1
    GROUPS, PER_GROUP, TOP_GROUPS = 8, 4, 4
    NTILE = T * TOP // ROWS + E8
    XROWS = T * TOP + ROWS
    NB = CT // SEQ
    BP = NB // 2
    LAG = 3
    V9 = DK + 1

    with ExitStack() as ctx:
        def sb(name, shape, dt):
            return ctx.enter_context(nc.sbuf_tensor(name, shape, dt))

        def sem(name):
            return ctx.enter_context(nc.semaphore(name))

        x_sb = sb("x_sb", [P, NT, P], F32)
        w1 = sb("w1", [P, 2, E8 * FC * P], F16)
        w2 = sb("w2", [P, 2, E8 * FC * P], F16)
        wgu_g = sb("wgu_g", [P, 2, NP * P], F16)
        wgu_u = sb("wgu_u", [P, 2, NP * P], F16)
        wdn = sb("wdn", [P, 2, NP * P], F16)
        watt = sb("watt", [P, 2, 4 * P], F16)
        wgate = sb("wgate", [P, 2, E8 + E32], F16)
        wt1 = sb("wt1", [P, FC * P], F16)
        wt2 = sb("wt2", [P, FC * P], F16)
        stage = sb("stage", [P, 2, 2048], F32)
        tern = sb("tern", [P, 2, FC * P], F32)
        tern_neg = sb("tern_neg", [P, 2, FC * P], F32)
        b1T = sb("b1T", [P, E8 * FC], F32)
        b2_bc = sb("b2_bc", [P, E8 * P], F32)
        wg_f32 = sb("wg_f32", [P, E8], F32)
        bg_bc = sb("bg_bc", [P, E8], F32)
        gbias_bc = sb("gbias_bc", [P, JT, E32], F32)
        bq_col = sb("bq_col", [P, 1], F32)
        bqs_col = sb("bqs_col", [P, 1], F32)
        bk_col = sb("bk_col", [P, 1], F32)
        bv_bc = sb("bv_bc", [P, P], F32)
        bv8 = sb("bv8", [P, NB * SEQ], F32)
        bo4 = sb("bo4", [P, JT, P], F32)
        fb1_col = sb("fb1_col", [P, FC], F32)
        fb2_4 = sb("fb2_4", [P, JT, P], F32)
        gates = sb("gates", [P, 4], F32)
        tg = sb("tg", [P, 4], F32)
        tgs = sb("tgs", [P, 4], F32)
        ident = sb("ident", [P, P], F32)
        ones = sb("ones", [P, P], F32)
        ones16 = sb("ones16", [P, CT], F16)
        ident16 = sb("ident16", [P, P], F16)
        below16 = sb("below16", [P, P], F16)
        unscale16 = sb("unscale16", [1, P], F16)
        tri = sb("tri", [P, 8, 8], F32)
        hm = sb("hm", [P, 4, 4], F32)
        headmask = sb("headmask", [P, 4], F32)
        sel = sb("sel", [2 * E32, PAIRS, 2, SEQ], F16)
        half_pow = sb("half_pow", [P, NT], F32)
        tern_sum = sb("tern_sum", [P, 2], F32)
        tern_hs = sb("tern_hs", [P, 2], F32)
        tern_nhs = sb("tern_nhs", [P, 2], F32)

        staged = [sem("staged0"), sem("staged1")]
        split_hi_done = sem("split_hi_done")
        split_lo_done = sem("split_lo_done")
        small_loaded = sem("small_loaded")
        tern_loaded = sem("tern_loaded")
        const_ready = sem("const_ready")
        pool_step = sem("pool_step")
        tern_abs_ready = sem("tern_abs_ready")
        tern_total_ready = sem("tern_total_ready")
        tern_ready = sem("tern_ready")
        tanh_ready = sem("tanh_ready")
        dve_chain = sem("dve_chain")

        nB, nC, nD = (Norm(n, sb, sem) for n in ("B", "C", "D"))
        cx = {}
        for s in ("C",):
            cx[s] = dict(f=sb(f"cx{s}_f", [P, CT], F32), hi=sb(f"cx{s}_hi", [P, CT], F16),
                         lo=sb(f"cx{s}_lo", [P, CT], F16), loaded=sem(f"cx{s}_loaded"),
                         hi_ready=sem(f"cx{s}_hi_ready"), lo_ready=sem(f"cx{s}_lo_ready"))
        rk_gt = sb("rk_gt", [P, JT, 8, 8], F32)
        rk_eq = sb("rk_eq", [P, JT, 8, 8], F32)
        rk = sb("rk", [P, JT, 8], F32)
        a_r = sb("a_r", [P, 2, FC, ROWS], F32)
        halves = stage[:, :, :].bitcast(F16)
        a_hh = halves[:, 0, 0:2 * FC * ROWS].rearrange("p (b k t) -> p b k t", b=2, k=FC)
        a_hl = halves[:, 0, 2 * FC * ROWS:].rearrange("p (b k t) -> p b k t", b=2, k=FC)
        a_yg = stage[:, 1, 0:TOP * CT].rearrange("p (k j d) -> p k j d", k=TOP, d=P)
        a_rows = sb("a_rows", [P, 4, 2, 2 * P], F16)
        a_xT = sb("a_xT", [P, 2, 2, ROWS], F16)
        a_y = sb("a_y", [P, 2, 2, P], F32)
        idx_x = sb("idx_x", [P, TOP, NT], F32)
        idx_y = sb("idx_y", [P, TOP, NT], F32)
        idx_now = sb("idx_now", [P, 2, TOP, JT], U32)
        a_tw = sb("a_tw", [P, TOP, NT], F32)
        a_v = sb("a_v", [P, TOP, NT], F32)
        a_e2 = sb("a_e2", [P, NT], F32)
        a_rec = sb("a_rec", [P, NT], F32)
        iota_t = sb("iota_t", [P, NTILE], I32)
        from8_i = sb("from8_i", [P, E8], I32)
        from8 = sb("from8", [P, E8], F32)
        iota_f = sb("iota_f", [P, NTILE], F32)
        a_small = sb("a_small", [P, 8, E8], F32)
        a_tab = sb("a_tab", [P, 3, NTILE], F32)
        tile_expert = sb("tile_expert", [1, NTILE], I32)
        tile_row = sb("tile_row", [1, NTILE], I32)
        tile_column = sb("tile_column", [1, NTILE], I32)
        a_scattered = [sem("a_scattered0"), sem("a_scattered1")]
        a_rows_loaded = [sem(f"a_rows_loaded{k}") for k in range(4)]
        a_y_stored = [sem("a_y_stored0"), sem("a_y_stored1")]
        a_gathered = sem("a_gathered")
        ctx_loaded = [sem("ctx_loaded0"), sem("ctx_loaded1")]
        x_part_loaded = [sem("x_part_loaded0"), sem("x_part_loaded1")]
        wg_loaded = sem("wg_loaded")
        zeros_stored = sem("zeros_stored")
        a_logit_ready = sem("a_logit_ready")
        a_chosen_ready = sem("a_chosen_ready")
        a_counts_ready = sem("a_counts_ready")
        a_shift_ready = sem("a_shift_ready")
        a_exp_ready = sem("a_exp_ready")
        a_idx_ready = sem("a_idx_ready")
        a_idx_now_ready = sem("a_idx_now_ready")
        a_table_ready = sem("a_table_ready")
        a_var_ready = sem("a_var_ready")
        a_rstd_ready = sem("a_rstd_ready")
        a_xn_ready = sem("a_xn_ready")
        a_xhi_ready = sem("a_xhi_ready")
        a_xlo_ready = sem("a_xlo_ready")
        a_T_ready = sem("a_T_ready")
        a_xT_ready = sem("a_xT_ready")
        a_h_ready = sem("a_h_ready")
        a_r_ready = sem("a_r_ready")
        a_hh_ready = sem("a_hh_ready")
        a_hl_ready = sem("a_hl_ready")
        a_o_ready = sem("a_o_ready")
        a_y_ready = sem("a_y_ready")
        a_weighed = sem("a_weighed")
        a_half_added = sem("a_half_added")
        a_x_done = sem("a_x_done")

        b_th = sb("b_th", [P, JT * E32], F32)
        b_sc = sb("b_sc", [P, JT, E32], F32)
        b_scb = sb("b_scb", [P, JT * GROUPS, 2, 2], F32)
        b_mx = sb("b_mx", [P, JT * GROUPS, 2], F32)
        b_mn = sb("b_mn", [P, JT * GROUPS, 2], F32)
        b_t1 = sb("b_t1", [P, JT * GROUPS], F32)
        b_t2 = sb("b_t2", [P, JT * GROUPS], F32)
        b_t3 = sb("b_t3", [P, JT * GROUPS], F32)
        b_gs = sb("b_gs", [P, JT, GROUPS], F32)
        b_gm = sb("b_gm", [P, JT, GROUPS], F32)
        b_masked = sb("b_masked", [P, JT, E32], F32)
        b_m8 = sb("b_m8", [P, JT, 8], F32)
        b_mr = sb("b_mr", [P, JT, E32], F32)
        b_ws = sb("b_ws", [P, JT, E32], F32)
        b_wsum = sb("b_wsum", [P, JT], F32)
        b_wrec = sb("b_wrec", [P, JT], F32)
        b_comb = sb("b_comb", [P, JT, E32], F32)
        b_cT = sb("b_cT", [2 * E32, CT], F16)
        b_silu = sb("b_silu", [P, 2, CT], F32)
        b_su = sb("b_su", [P, 2, CT], F32)
        b_act = sb("b_act", [P, 2, CT], F32)
        b_ah = sb("b_ah", [P, LAG + 1, CT], F16)
        b_al = sb("b_al", [P, LAG + 1, CT], F16)
        b_yT = sb("b_yT", [P, CT], F32)
        b_route_ready = sem("b_route_ready")
        b_score_ready = sem("b_score_ready")
        b_comb_ready = sem("b_comb_ready")
        b_combT_ready = sem("b_combT_ready")
        b_ch_ready = sem("b_ch_ready")
        b_cl_ready = sem("b_cl_ready")
        b_g_ready = sem("b_g_ready")
        b_gu_ready = sem("b_gu_ready")
        b_silu_ready = sem("b_silu_ready")
        b_u_used = sem("b_u_used")
        b_act_ready = sem("b_act_ready")
        b_ah_ready = sem("b_ah_ready")
        b_al_ready = sem("b_al_ready")
        b_down_done = sem("b_down_done")
        b_yT_ready = sem("b_yT_ready")
        b_y_ready = sem("b_y_ready")
        b_x_done = sem("b_x_done")

        c_q = sb("c_q", [P, CT], F32)
        c_qh = sb("c_qh", [P, CT], F16)
        c_ql = sb("c_ql", [P, CT], F16)
        c_k = sb("c_k", [P, CT], F32)
        c_kh = sb("c_kh", [P, CT], F16)
        c_kl = sb("c_kl", [P, CT], F16)
        c_km = sb("c_km", [P, 2, 4, CT], F16)
        c_vbd = sb("c_vbd", [P, NB, HEADS // 2, 2, V9], F32)
        c_max = sb("c_max", [P, HEADS], F32)
        w1_f32 = w1[:, :, :].bitcast(F32)
        c_p = w1_f32[:, 0, :].rearrange("p (b n) -> p b n", b=2)
        c_pT = w1_f32[:, 1, :].rearrange("p (b h t) -> p b h t", b=2, t=P)
        c_rec = sb("c_rec", [P, HEADS], F32)
        a_r4 = a_r[:, :, :, :].rearrange("p b (k m) t -> p (b k) (m t)", m=2)
        c_on = a_r4[:, 0, :].rearrange("p (j h k) -> p j h k", h=HEADS, k=DK)
        c_oh, c_ol = tern_neg[:, 0, 0:CT // 2].bitcast(F16), tern_neg[:, 0, CT // 2:].bitcast(F16)
        c_y = a_r4[:, 1, :].rearrange("p (j d) -> p j d", d=P)
        c_qp_ready = sem("c_qp_ready")
        c_q_ready = sem("c_q_ready")
        c_ql_ready = sem("c_ql_ready")
        c_kp_ready = sem("c_kp_ready")
        c_k_ready = sem("c_k_ready")
        c_km_ready = sem("c_km_ready")
        c_vp_ready = sem("c_vp_ready")
        c_v_ready = sem("c_v_ready")
        c_s_ready = sem("c_s_ready")
        c_shift_ready = sem("c_shift_ready")
        c_exp_ready = sem("c_exp_ready")
        c_pT_ready = sem("c_pT_ready")
        c_pT_copied = sem("c_pT_copied")
        c_o_ready = sem("c_o_ready")
        c_on_ready = sem("c_on_ready")
        c_oT_ready = sem("c_oT_ready")
        c_oh_ready = sem("c_oh_ready")
        c_ol_ready = sem("c_ol_ready")
        c_y_ready = sem("c_y_ready")
        c_y_used = sem("c_y_used")
        c_x_done = sem("c_x_done")

        d_g = w2[:, 0, :].bitcast(F32).rearrange("p (k t) -> p k t", k=FC)
        d_gh = w2[:, 1, 0:FC * CT].rearrange("p (k t) -> p k t", k=FC)
        d_gl = w2[:, 1, FC * CT:].rearrange("p (k t) -> p k t", k=FC)
        d_y = a_r4[:, 2, :].rearrange("p (j d) -> p j d", d=P)
        x_out = a_r4[:, 3, :].rearrange("p (j d) -> p j d", d=P)
        d_h_ready = sem("d_h_ready")
        d_gh_ready = sem("d_gh_ready")
        d_gl_ready = sem("d_gl_ready")
        d_y_ready = sem("d_y_ready")
        d_y_used = sem("d_y_used")
        d_x_ready = sem("d_x_ready")
        stored = sem("stored")

        H = 2048
        ctx_half = (a_r[:, :, :, :].rearrange("p b k t -> p (b k t)"),
                    c_km[:, :, :, :].rearrange("p h r t -> p (h r t)").bitcast(F32))

        def scratch(buf, n):
            w = NT * E8
            v = buf[:, :, :].rearrange("p b t -> p (b t)")[:, n * w:(n + 1) * w]
            return v.rearrange("p (t e) -> p t e", e=E8)

        a_logits, a_rest, a_m1, a_m2 = (scratch(b_su, n) for n in range(4))
        a_scan0, a_scan1, a_pos, a_tmp = (scratch(b_act, n) for n in range(4))
        a_m16 = b_ah[:, 0, 0:NT * E8].rearrange("p (t e) -> p t e", e=E8)
        a_xn = b_silu[:, 0, :].rearrange("p (j d) -> p j d", d=P)
        a_tt = c_q[:, 0:NTILE * E8].rearrange("p (k e) -> p k e", e=E8)
        a_tn = c_k[:, 0:16 * E8].rearrange("p (e m) -> p e m", m=16)
        a_tg = c_k[:, 16 * E8:16 * E8 + E8 * E8].rearrange("p (g h) -> p g h", h=E8)
        a_hl16 = a_rows[:, :, :, :].rearrange("p s h d -> p (s h) d").rearrange("p (s j) d -> p s j d", s=2)
        a_stats = nB.xn[:, :, :].rearrange("p j d -> p (j d)")[:, 0:NT * 6].rearrange("p (t s) -> p t s", s=6)
        a_mv = sb("a_mv", [P, NT, 2], F32)
        a_ve = sb("a_ve", [P, NT], F32)
        a_rstd = sb("a_rstd", [P, NT], F32)
        zeros = a_y[:, 0, :, :].rearrange("p h d -> p (h d)").bitcast(F16)

        x_slots = nc.dram_tensor("x_slots", (XROWS, 2 * P), F16).ap()
        y_slots = nc.dram_tensor("y_slots", (NTILE * ROWS, P), F32).ap()

        ps4 = ctx.enter_context(nc.psum_tensor("ps4", [P, 4, 512], F32))
        ps2 = ctx.enter_context(nc.psum_tensor("ps2", [P, 2, 512], F32))
        ps_out = ctx.enter_context(nc.psum_tensor("ps_out", [P, 512], F32))
        ps_misc = ctx.enter_context(nc.psum_tensor("ps_misc", [P, 512], F32))

        x_dram = x_d.rearrange("(n p) d -> p n d", p=P)
        out_dram = out_d.rearrange("(n p) d -> p n d", p=P)

        def cols(w, a, n):
            return w[:, 0, a:a + n], w[:, 1, a:a + n]

        WG0, WA0, WS0 = 0, E8 + E32, E8 + E32 + 4 * P
        JOBS = [
            [(cols(w1, 0, H), w1_d[:, 0:H])], [(cols(w1, H, H), w1_d[:, H:2 * H])],
            [(cols(w2, 0, H), w2_d[:, 0:H])], [(cols(w2, H, H), w2_d[:, H:2 * H])],
            [(cols(wgate, E8, E32), gate_w_d),
             (cols(watt, 0, P), wq_d), (cols(watt, P, P), wk_d), (cols(watt, 2 * P, P), wv_d),
             (cols(watt, 3 * P, P), wo_d), (cols(wgu_g, PAIRS * P, P), sh_gate_d),
             (cols(wgu_u, PAIRS * P, P), sh_up_d), (cols(wdn, PAIRS * P, P), sh_down_d)],
            [(cols(wgu_g, 0, H), w_gate_d)], [(cols(wgu_u, 0, H), w_up_d)], [(cols(wdn, 0, H), w_down_d)],
        ]
        SMALL = [
            (b1T[:, :], b1_d), (b2_bc[:, :], b2_d.partition_broadcast(P)),
            (bq_col[:, :], bq_d), (bk_col[:, :], bk_d), (fb1_col[:, :], fb1_d),
            (gates[:, 0:2], g_xattn_d.partition_broadcast(P)), (gates[:, 2:4], g_ffn_d.partition_broadcast(P)),
        ] + [(gbias_bc[:, j, :], gate_bias_d.partition_broadcast(P)) for j in range(JT)] \
          + [(bv_bc[:, :], bv_d.partition_broadcast(P))] \
          + [(bo4[:, j, :], bo_d.partition_broadcast(P)) for j in range(JT)] \
          + [(fb2_4[:, j, :], fb2_d.partition_broadcast(P)) for j in range(JT)]
        STATS = (0, 3), (3, NC)
        N_CONST = 14
        GX0, GF0, GX1, GF1 = 0, 2, 1, 3

        def xt(c, j):
            return x_sb[:, bass.ds(c * JT + j, 1), :].rearrange("p a d -> p (a d)")

        def xchunk(c):
            return x_sb[:, bass.ds(c * JT, JT), :]

        SLOTS = dict(ctx=4, norm_C=1, T_C=6, q=8, k=10, norm_D=7, T_D=13, norm_B=16,
                     weigh=13)
        SLOTS_ALONE = dict(SLOTS, ctx=0, norm_C=0, T_C=4, q=6, k=0, norm_D=1, T_D=9)

        def slots(i):
            return SLOTS if has(i) else SLOTS_ALONE

        LOOP = (3, NC - 1)

        def has(c):
            return not isinstance(c, int) or 0 <= c < NC

        def upto(c):
            return max(0, min(c, NC)) if isinstance(c, int) else c

        def run_pipeline(eng, body):
            for i in range(LOOP[0]):
                body(i)
            with eng.Fori(*LOOP) as i:
                body(i)
            for i in range(LOOP[1], NC + 2):
                body(i)

        PER = 4

        EARLY = dict(weigh=1, combine=2, norm=3, normalise=6)

        def late_weights(i):
            return isinstance(i, int) and i in (0, 1)

        def is_first(k):
            return isinstance(k, int) and k == 0

        def tile_exists(k):
            return not isinstance(k, int) or k < NTILE

        def run_tiles(eng, body):
            for m in range(PER):
                body(0, m, m)
            with eng.Fori(1, NTILE // PER - 1) as i:
                for m in range(PER):
                    body(i, i * PER + m, m)
            last = NTILE // PER - 1
            for m in range(PER):
                body(last, last * PER + m, m)

        nB.used = (b_gu_ready, NP)
        nC.used, nD.used = (c_qp_ready, 1), (d_h_ready, FC)
        cx["C"]["used"] = (c_vp_ready, 1)

        T16 = [b[:, :].bitcast(F16)[:, 0:2 * ROWS].rearrange("p (h t) -> p h t", h=2) for b in (ps_out, ps_misc)]

        def h_bank(m, f):
            return ps4[:, 2 * (m % 2) + f // 2, (f % 2) * ROWS:(f % 2 + 1) * ROWS]

        block = ctx.enter_context(nc.Block())

        @block.sync
        def _(sp):
            sp.dma_start(wg_f32[:, :], wg_d).then_inc(wg_loaded, 16)
            sp.dma_start(bg_bc[:, :], bg_d.partition_broadcast(P)).then_inc(wg_loaded, 16)
            for h in range(2):
                sp.dma_start(ctx_half[h], ctxT_d[:, h * H:(h + 1) * H]).then_inc(ctx_loaded[h], 16)
            for part, (first, last) in enumerate(STATS):
                t = slice(first * JT, last * JT)
                sp.dma_start(x_sb[:, t, :], x_dram[:, t, :]).then_inc(x_part_loaded[part], 16)
            with nc.allow_non_contiguous_dma(reason="small columns and broadcasts, once"):
                for dst, src in SMALL:
                    sp.dma_start(dst, src).then_inc(small_loaded, 16)
            for n, job in enumerate(JOBS):
                if n >= 2:
                    sp.wait_ge(split_hi_done, n - 1)
                    sp.wait_ge(split_lo_done, n - 1)
                at = 0
                for (hi, _), src in job:
                    w = hi.shape[1]
                    sp.dma_start(stage[:, n % 2, at:at + w], src).then_inc(staged[n % 2], 16)
                    at += w
            sp.dma_start(tern[:, 0, :], f1_d).then_inc(tern_loaded, 16)
            sp.dma_start(tern[:, 1, :], f2_d).then_inc(tern_loaded, 16)

            sp.wait_ge(const_ready, N_CONST)
            sp.dma_start(x_slots[T * TOP:XROWS, :].rearrange("(p h) d -> p (h d)", p=P), zeros)\
              .then_inc(zeros_stored, 16)
            sp.wait_ge(zeros_stored, 16)
            for half in range(2):
                sp.wait_ge(a_scattered[half], 16 * TOP * JT * NC // 2)
            sp.wait_ge(a_table_ready, 1)

            def load_rows(turn, k, m):
                at_least(sp, a_T_ready, k - PER + 1)
                row = sp.value_load(tile_row[0:1, bass.ds(k, 1)], min_val=0, max_val=T * TOP)
                sp.dma_start(a_rows[:, m, :, :], x_slots[bass.ds(row, ROWS), :].rearrange("(h p) d -> p h d", p=P))\
                  .then_inc(a_rows_loaded[m], 16)

            run_tiles(sp, load_rows)

            def load_ctx(s, c):
                at_least(sp, cx[s]["hi_ready"], c)
                at_least(sp, cx[s]["lo_ready"], c)
                sp.dma_start(cx[s]["f"][:, :], ctxT_d[:, bass.ds(c * CT, CT)]).then_inc(cx[s]["loaded"], 16)

            def store(c):
                sp.wait_ge(d_x_ready, c + 1)
                sp.dma_start(out_dram[:, bass.ds(c * JT, JT), :], x_out[:, :, :]).then_inc(stored, 16)

            load_ctx("C", 0)
            load_ctx("C", 1)
            with sp.Fori(2, NC) as i:
                load_ctx("C", i)
                store(i - 2)
            for c in (NC - 2, NC - 1):
                store(c)
            sp.wait_ge(stored, 16 * NC)

        @block.gpsimd
        def _(pool):
            steps = [0]

            def step(ins):
                ins.then_inc(pool_step, 1)
                steps[0] += 1
                pool.wait_ge(pool_step, steps[0])

            step(pool.memset(a_y[:, 0, :, :], 0.0))
            step(pool.iota(iota_t[:, :], [[ROWS, NTILE]], base=0, channel_multiplier=0))
            pool.tensor_copy(iota_f[:, :], iota_t[:, :]).then_inc(const_ready, 1)
            step(pool.iota(from8_i[:, :], [[-1, E8]], base=E8, channel_multiplier=0))
            pool.tensor_copy(from8[:, :], from8_i[:, :]).then_inc(const_ready, 1)
            step(pool.memset(below16[:, :], 1.0))
            pool.affine_select(out=below16[:, :], in_=below16[:, :], compare_op=ALU.is_gt, fill=0.0, base=0,
                               pattern=[[1, P]], channel_multiplier=-1).then_inc(const_ready, 1)
            step(pool.memset(ident16[:, :], 0.0))
            pool.affine_select(out=ident16[:, :], in_=ident16[:, :], compare_op=ALU.not_equal, fill=1.0, base=0,
                               pattern=[[-1, P]], channel_multiplier=1).then_inc(const_ready, 1)
            step(pool.memset(ident[:, :], 0.0))
            pool.affine_select(out=ident[:, :], in_=ident[:, :], compare_op=ALU.not_equal, fill=1.0, base=0,
                               pattern=[[-1, P]], channel_multiplier=1).then_inc(const_ready, 1)
            pool.memset(ones[:, :], 1.0).then_inc(const_ready, 1)
            pool.memset(ones16[:, :], 1.0).then_inc(const_ready, 1)
            pool.memset(unscale16[:, :], 1.0 / WSCALE).then_inc(const_ready, 1)
            pool.memset(half_pow[:, :], -0.5).then_inc(const_ready, 1)
            step(pool.memset(tri[:, :, :], 1.0))
            pool.affine_select(out=tri[:, :, :], in_=tri[:, :, :], compare_op=ALU.is_gt, fill=0.0, base=0,
                               pattern=[[1, 8], [-1, 8]], channel_multiplier=0).then_inc(const_ready, 1)
            v = hm[:, :, :]
            step(pool.memset(v, 1.0))
            step(pool.affine_select(out=v, in_=v, compare_op=ALU.is_ge, fill=0.0, base=0,
                                    pattern=[[-32, 4], [-8, 4]], channel_multiplier=1))
            step(pool.affine_select(out=v, in_=v, compare_op=ALU.is_ge, fill=0.0, base=7,
                                    pattern=[[32, 4], [8, 4]], channel_multiplier=-1))
            step(pool.tensor_tensor(hm[:, 0:2, :], hm[:, 0:2, :], hm[:, 2:4, :], ALU.add))
            pool.tensor_tensor(headmask[:, :], hm[:, 0, :], hm[:, 1, :], ALU.add).then_inc(const_ready, 1)
            step(pool.memset(sel[:, :, :, :], 0.0))
            step(pool.affine_select(out=sel[:, :, :, :], in_=sel[:, :, :, :], compare_op=ALU.not_equal,
                                    fill=1.0 / WSCALE, base=0, pattern=[[-2, PAIRS], [-1, 2], [0, SEQ]],
                                    channel_multiplier=1))
            pool.affine_select(out=sel[:, :, :, :], in_=sel[:, :, :, :], compare_op=ALU.not_equal,
                               fill=1.0 / WSCALE, base=-E32, pattern=[[-2, PAIRS], [-1, 2], [0, SEQ]],
                               channel_multiplier=1).then_inc(const_ready, 1)
            step(pool.memset(c_vbd[:, :, :, :, :], 0.0))
            pool.memset(c_vbd[0:SEQ, :, :, 0, DK:V9], 1.0).then_inc(const_ready, 1)
            pool.memset(c_vbd[SEQ:P, :, :, 1, DK:V9], 1.0).then_inc(const_ready, 1)

            def rstd(n, c):
                pool.wait_ge(n.var_ready, c + 1)
                pool.tensor_tensor(n.rstd[:, :], n.var_eps[:, :], half_pow[:, 0:JT], ALU.pow)\
                    .then_inc(n.rstd_ready, 1)
                pool.wait_ge(n.rstd_ready, c + 1)
                pool.tensor_tensor(n.offset[:, :], n.neg_mean[:, :], n.rstd[:, :], ALU.mult)\
                    .then_inc(n.offset_ready, 1)

            def low_part(c, e):
                pool.wait_ge(b_ah_ready, NP * c + e + 1)
                at_least(pool, b_down_done, NP * c + max(e - LAG, 0))
                pool.tensor_tensor(b_al[:, e % (LAG + 1), :], b_act[:, e % 2, :], b_ah[:, e % (LAG + 1), :],
                                   ALU.subtract).then_inc(b_al_ready, 1)

            pool.wait_ge(const_ready, N_CONST)

            indices = Chain(pool, a_idx_now_ready)

            def take_indices(c, slot, idx, ready, count):
                indices.restart()
                at_least(pool, ready, count)
                indices(pool.tensor_copy(idx_now[:, slot, :, :], idx[:, :, bass.ds(c * JT, JT)]))
                indices.sync()

            def a_rstd_tiles(part):
                t = slice(STATS[part][0] * JT, STATS[part][1] * JT)
                pool.wait_ge(a_var_ready, part + 1)
                pool.tensor_tensor(a_rstd[:, t], a_ve[:, t], half_pow[:, t], ALU.pow).then_inc(a_rstd_ready, 1)

            def scatter(c, slot):
                take_indices(c, slot, idx_x, a_xlo_ready, c + 1)
                for j in range(JT):
                    for k in range(TOP):
                        at = bass.IndirectOffsetOnAxis(ap=idx_now[:, slot, k, j:j + 1], axis=0)
                        pool.indirect_dma_start(x_slots, at, a_hl16[:, slot, j, :], None)\
                            .then_inc(a_scattered[slot], 16)

            a_rstd_tiles(0)
            pool.wait_ge(a_idx_ready, 1)
            scatter(0, 0)
            a_rstd_tiles(1)
            scatter(1, 1)
            with pool.Fori(1, NC // 2) as i:
                for slot in range(2):
                    scatter(i * 2 + slot, slot)

            def store_tile(turn, k, m):
                pool.wait_ge(a_y_ready, k + 1)
                pool.dma_start(y_slots[bass.ds(k * ROWS, ROWS), :].rearrange("(h p) d -> p h d", p=P),
                               a_y[:, m % 2, :, :]).then_inc(a_y_stored[m % 2], 16)

            run_tiles(pool, store_tile)
            for half in range(2):
                pool.wait_ge(a_y_stored[half], 16 * NTILE // 2)

            def gather(c, k, j):
                if (k, j) == (0, 0):
                    take_indices(c, 0, idx_y, a_x_done, c)
                at = bass.IndirectOffsetOnAxis(ap=idx_now[:, 0, k, j:j + 1], axis=0)
                pool.indirect_dma_start(a_yg[:, k, j, :], None, y_slots, at).then_inc(a_gathered, 16)

            def gelu_lo(c, k):
                pool.wait_ge(d_gh_ready, FC * c + k + 1)
                at_least(pool, d_y_ready, c)
                pool.tensor_tensor(d_gl[:, k, :], d_g[:, k, :], d_gh[:, k, :], ALU.subtract).then_inc(d_gl_ready, 1)

            for j in range(JT):
                for k in range(TOP):
                    gather(0, k, j)
            rstd(nB, 0)
            for j in range(JT):
                for k in range(TOP):
                    gather(1, k, j)

            def body(i):
                S = slots(i)
                for e in range(NP):
                    if has(i):
                        low_part(i, e)
                    if e == S["norm_C"] and has(i - 1):
                        rstd(nC, i - 1)
                    if e == S["norm_D"] and has(i - 2):
                        rstd(nD, i - 2)
                    if is_first(i) and e == EARLY["norm"]:
                        rstd(nB, 1)
                    if 2 <= e < 2 + TOP * JT and has(i + 1) and not is_first(i):
                        gather(i + 1, (e - 2) % TOP, (e - 2) // TOP)
                if has(i + 1) and not is_first(i):
                    rstd(nB, i + 1)
                if has(i - 2):
                    for k in range(FC):
                        gelu_lo(i - 2, k)

            run_pipeline(pool, body)

        @block.scalar
        def _(act):
            def split_hi(n):
                job = JOBS[n]
                act.wait_ge(staged[n % 2], 16 * sum(len(JOBS[m]) for m in range(n % 2, n + 1, 2)))
                at = 0
                for (hi, _), src in job:
                    w = hi.shape[1]
                    last = act.activation(hi, stage[:, n % 2, at:at + w], ACT.Copy, scale=WSCALE)
                    at += w
                last.then_inc(split_hi_done, 1)

            for c in range(NC):
                act.wait_ge(a_xn_ready, c + 1)
                if c >= 2:
                    act.wait_ge(a_scattered[c % 2], 16 * TOP * JT * (c // 2))
                act.activation(a_hl16[:, c % 2, :, 0:P], a_xn[:, :, :], ACT.Copy).then_inc(a_xhi_ready, 1)
                if c == 0:
                    act.wait_ge(a_shift_ready, 1)
                    act.activation(a_e2[:, :], a_e2[:, :], ACT.Exp).then_inc(a_exp_ready, 1)
                if c == 1:
                    split_hi(0)
                if c >= 1:
                    split_hi(c)
            act.wait_ge(small_loaded, 16 * len(SMALL))
            act.activation(tg[:, :], gates[:, :], ACT.Tanh).then_inc(tanh_ready, 1)
            act.activation(bqs_col[:, :], bq_col[:, :], ACT.Copy, scale=DK ** -0.5).then_inc(tanh_ready, 1)
            act.wait_ge(tanh_ready, 2)

            def normalise(n, c):
                act.wait_ge(n.offset_ready, c + 1)
                at_least(act, n.xT_ready, c)
                for j in range(JT):
                    last = act.activation(n.xn[:, j, :], xt(c, j), ACT.Identity, bias=n.offset[:, j:j + 1],
                                          scale=n.rstd[:, j:j + 1])
                last.then_inc(n.xn_ready, 1)

            def norm_hi(n, c):
                act.wait_ge(n.xT_ready, c + 1)
                at_least(act, n.used[0], n.used[1] * c)
                at_least(act, n.lo_ready, c)
                act.activation(n.hi[:, :], ps_misc[:, :], ACT.Copy).then_inc(n.hi_ready, 1)

            def ctx_hi(s, c):
                act.wait_ge(cx[s]["loaded"], 16 * (c + 1))
                at_least(act, cx[s]["used"][0], cx[s]["used"][1] * c)
                at_least(act, cx[s]["lo_ready"], c)
                act.activation(cx[s]["hi"][:, :], cx[s]["f"][:, :], ACT.Copy).then_inc(cx[s]["hi_ready"], 1)

            def copy_T(k, m):
                act.wait_ge(a_T_ready, k + 1)
                at_least(act, a_h_ready, 2 * (k - 1))
                act.activation(a_xT[:, m % 2, :, :], T16[m % 2], ACT.Copy).then_inc(a_xT_ready, 1)

            def relu(turn, k, m):
                if is_first(k):
                    copy_T(0, 0)
                if tile_exists(k + 1):
                    copy_T(k + 1, m + 1)
                expert = act.value_load(tile_expert[0:1, bass.ds(k, 1)], min_val=0, max_val=E8 - 1)
                at_least(act, a_hh_ready, k - 1)
                at_least(act, a_hl_ready, k - 1)
                for f in range(FC):
                    if f % 2 == 0:
                        act.wait_ge(a_h_ready, k * 2 + (f // 2 + 1))
                    act.activation(a_r[:, m % 2, f, :], h_bank(m, f), ACT.Relu,
                                   bias=b1T[:, bass.ds(expert * FC + f, 1)], scale=1.0 / WSCALE)\
                       .then_inc(a_r_ready, 1)

            run_tiles(act, relu)
            act.wait_ge(a_o_ready, NTILE)

            def weigh(c, k):
                act.wait_ge(a_gathered, 16 * TOP * JT * (c + 1))
                for j in range(JT):
                    last = act.activation(a_yg[:, k, j, :], a_yg[:, k, j, :], ACT.Copy,
                                          scale=a_tw[:, k, bass.ds(c * JT + j, 1)])
                last.then_inc(a_weighed, 1)

            def score(c):
                act.wait_ge(b_route_ready, c + 1)
                at_least(act, b_comb_ready, c)
                act.activation(b_th[:, :], ps_misc[:, 0:JT * E32], ACT.Tanh, scale=0.5 / WSCALE)\
                   .then_inc(b_score_ready, 1)

            def comb_hi(c):
                act.wait_ge(b_combT_ready, c + 1)
                at_least(act, b_gu_ready, NP * c)
                at_least(act, b_cl_ready, c)
                act.activation(b_cT[0:E32, :], ps_misc[0:E32, :], ACT.Copy, scale=ROUTED_SCALE)\
                   .then_inc(b_ch_ready, 1)

            def silu(c, e):
                act.wait_ge(b_g_ready, NP * c + e + 1)
                at_least(act, b_u_used, NP * c + max(e - 1, 0))
                act.activation(b_silu[:, e % 2, :], ps4[:, e % 2, :], ACT.Silu, scale=1.0 / WSCALE)\
                   .then_inc(b_silu_ready, 1)

            def act_hi(c, e):
                act.wait_ge(b_act_ready, NP * c + e + 1)
                at_least(act, b_down_done, NP * c + max(e - LAG, 0))
                act.activation(b_ah[:, e % (LAG + 1), :], b_act[:, e % 2, :], ACT.Copy).then_inc(b_ah_ready, 1)

            def b_copy(c):
                act.wait_ge(b_down_done, NP * (c + 1))
                at_least(act, b_y_ready, c)
                act.activation(b_yT[:, :], ps_out[:, :], ACT.Copy).then_inc(b_yT_ready, 1)

            def query(c):
                act.wait_ge(c_qp_ready, c + 1)
                at_least(act, c_ql_ready, c)
                at_least(act, c_s_ready, BP * c)
                scale = DK ** -0.5 / WSCALE
                act.activation(c_q[:, :], ps_misc[:, :], ACT.Identity, bias=bqs_col[:, 0:1], scale=scale)
                act.activation(c_qh[:, :], ps_misc[:, :], ACT.Identity, bias=bqs_col[:, 0:1], scale=scale)\
                   .then_inc(c_q_ready, 1)

            def key(c):
                act.wait_ge(c_kp_ready, c + 1)
                at_least(act, c_km_ready, c)
                act.activation(c_k[:, :], ps_misc[:, :], ACT.Identity, bias=bk_col[:, 0:1], scale=1.0 / WSCALE)
                act.activation(c_kh[:, :], ps_misc[:, :], ACT.Identity, bias=bk_col[:, 0:1],
                               scale=1.0 / WSCALE).then_inc(c_k_ready, 1)

            def exps(c, p):
                act.wait_ge(c_shift_ready, BP * c + p + 1)
                act.activation(c_p[:, p % 2, :], c_p[:, p % 2, :], ACT.Exp).then_inc(c_exp_ready, 1)

            def probs_copy(c, p):
                act.wait_ge(c_pT_ready, BP * c + p + 1)
                at_least(act, c_o_ready, BP * c + p - 1)
                act.activation(c_pT[:, p % 2, :, :], ps2[:, :, :].rearrange("p a (h t) -> p (a h) t", t=P),
                               ACT.Copy).then_inc(c_pT_copied, 1)

            def o_hi(c):
                act.wait_ge(c_oT_ready, c + 1)
                at_least(act, c_y_ready, c)
                at_least(act, c_ol_ready, c)
                act.activation(c_oh[:, :], ps_misc[:, :], ACT.Copy).then_inc(c_oh_ready, 1)

            def gelu(c, k):
                act.wait_ge(d_h_ready, FC * c + k + 1)
                at_least(act, d_gl_ready, FC * (c - 1) + k + 1)
                at_least(act, d_y_ready, c)
                act.activation(d_g[:, k, :], ps4[:, k, :], ACT.Gelu, bias=fb1_col[:, k:k + 1])
                act.activation(d_gh[:, k, :], ps4[:, k, :], ACT.Gelu, bias=fb1_col[:, k:k + 1])\
                   .then_inc(d_gh_ready, 1)

            for k in range(TOP):
                weigh(0, k)
            normalise(nB, 0)
            norm_hi(nB, 0)
            score(0)

            def body(i):
                B, C, D = i, i - 1, i - 2
                S = slots(i)
                if late_weights(i):
                    comb_hi(B)
                for e in range(NP):
                    if has(B):
                        silu(B, e)
                        if e >= 1:
                            act_hi(B, e - 1)
                    if has(C):
                        if e == S["ctx"]:
                            ctx_hi("C", C)
                        if e == S["norm_C"] + 2:
                            normalise(nC, C)
                        if e == S["T_C"]:
                            norm_hi(nC, C)
                        if e == S["q"]:
                            query(C)
                        if e == S["k"]:
                            key(C)
                    if has(D):
                        if e == S["norm_D"] + 2:
                            normalise(nD, D)
                        if e == S["T_D"]:
                            norm_hi(nD, D)
                    if is_first(i):
                        if e in (EARLY["weigh"], EARLY["weigh"] + 1):
                            weigh(1, e - EARLY["weigh"])
                        if e == EARLY["normalise"]:
                            normalise(nB, 1)
                    elif has(B + 1) and e in (S["weigh"], S["weigh"] + 1):
                        weigh(B + 1, e - S["weigh"])
                if has(B):
                    act_hi(B, NP - 1)
                    b_copy(B)
                if has(C):
                    exps(C, 0)
                if has(B + 1) and not is_first(i):
                    normalise(nB, B + 1)
                if has(C):
                    exps(C, 1)
                    probs_copy(C, 0)
                if has(B + 1):
                    norm_hi(nB, B + 1)
                if has(C):
                    exps(C, 2)
                    probs_copy(C, 1)
                if has(B + 1):
                    score(B + 1)
                if has(C):
                    exps(C, 3)
                    probs_copy(C, 2)
                    probs_copy(C, 3)
                if has(D):
                    gelu(D, 0)
                    gelu(D, 1)
                if has(B + 1) and not late_weights(B + 1):
                    comb_hi(B + 1)
                if has(D):
                    gelu(D, 2)
                    gelu(D, 3)
                if has(C):
                    o_hi(C)

            run_pipeline(act, body)

        @block.vector
        def _(dve):
            chain = Chain(dve, dve_chain)
            TT, TS, STT = dve.tensor_tensor, dve.tensor_scalar, dve.scalar_tensor_tensor

            def split_lo(n):
                dve.wait_ge(split_hi_done, n + 1)
                at = 0
                for (hi, lo), src in JOBS[n]:
                    w = hi.shape[1]
                    last = STT(out=lo, in0=stage[:, n % 2, at:at + w], scalar=WSCALE, in1=hi, op0=ALU.mult,
                               op1=ALU.subtract)
                    at += w
                last.then_inc(split_lo_done, 1)

            def ternary():
                dve.wait_ge(tern_loaded, 32)
                dve.tensor_reduce(tern_sum[:, :], tern[:, :, :], AX.X, ALU.add, apply_absolute_value=True)\
                   .then_inc(tern_abs_ready, 1)
                dve.wait_ge(tern_total_ready, 1)
                chain(TS(tern_hs[:, :], ps_misc[:, 0:2], 1.0 / (P * FC * P), 1e-8, ALU.mult, ALU.max))
                chain.sync()
                chain(TS(tern_nhs[:, :], tern_hs[:, :], -0.5, None, ALU.mult))
                chain.sync()
                chain(TS(tern_hs[:, :], tern_nhs[:, :], -1.0, None, ALU.mult))
                chain.sync()
                for k in range(2):
                    chain(TS(tern_neg[:, k, :], tern[:, k, :], tern_nhs[:, k:k + 1], None, ALU.is_lt))
                chain.sync()
                for k, w in enumerate((wt1, wt2)):
                    STT(out=w[:, :], in0=tern[:, k, :], scalar=tern_hs[:, k:k + 1], in1=tern_neg[:, k, :],
                        op0=ALU.is_gt, op1=ALU.subtract).then_inc(tern_ready, 1)

            def norm(n, c):
                for j in range(JT):
                    chain(dve.bn_stats(n.stats[:, j, :], xt(c, j)))
                chain.sync()
                at_least(dve, n.xn_ready, c)
                for j in range(JT):
                    chain(dve.bn_aggr(n.mean_var[:, j, :], n.stats[:, j, :]))
                chain.sync()
                TS(n.neg_mean[:, :].unsqueeze(2), n.mean_var[:, :, 0:1], -1.0, None, ALU.mult)
                TS(n.var_eps[:, :].unsqueeze(2), n.mean_var[:, :, 1:2], EPS, None, ALU.add)\
                    .then_inc(n.var_ready, 1)

            def norm_lo(n, c):
                dve.wait_ge(n.hi_ready, c + 1)
                at_least(dve, n.used[0], n.used[1] * c)
                TT(n.lo[:, :], ps_misc[:, :], n.hi[:, :], ALU.subtract).then_inc(n.lo_ready, 1)

            def ctx_lo(s, c):
                dve.wait_ge(cx[s]["hi_ready"], c + 1)
                at_least(dve, cx[s]["used"][0], cx[s]["used"][1] * c)
                TT(cx[s]["lo"][:, :], cx[s]["f"][:, :], cx[s]["hi"][:, :], ALU.subtract)\
                    .then_inc(cx[s]["lo_ready"], 1)

            def rank8(s):
                shape = [P, JT, 8, 8]
                gt, eq, out = rk_gt, rk_eq, rk
                other, own = s.unsqueeze(2).to_broadcast(shape), s.unsqueeze(3).to_broadcast(shape)
                chain(TT(gt[:, :, :, :], other, own, ALU.is_gt))
                chain(TT(eq[:, :, :, :], other, own, ALU.is_equal))
                chain.sync()
                chain(TT(eq[:, :, :, :], eq[:, :, :, :], tri[:, :, :].unsqueeze(1).to_broadcast(shape),
                         ALU.mult))
                chain.sync()
                chain(TT(gt[:, :, :, :], gt[:, :, :, :], eq[:, :, :, :], ALU.add))
                chain.sync()
                chain(dve.tensor_reduce(out[:, :, :], gt[:, :, :, :], AX.X, ALU.add))
                chain.sync()

            ALL = [P, NT, E8]

            def a_choose():
                dve.wait_ge(a_logit_ready, 1)
                dve.wait_ge(wg_loaded, 32)
                chain(TT(a_logits, ps_out[:, 0:NT * E8].rearrange("p (t e) -> p t e", e=E8),
                         bg_bc[:, :].unsqueeze(1).to_broadcast(ALL), ALU.add))
                chain.sync()
                rest = a_logits
                for n, mask in enumerate((a_m1, a_m2)):
                    best = a_v[:, n, :]
                    chain(dve.tensor_reduce(best, rest, AX.X, ALU.max))
                    chain.sync()
                    chain(TT(mask, rest, best.unsqueeze(2).to_broadcast(ALL), ALU.is_equal))
                    chain.sync()
                    chain(TT(mask, mask, from8[:, :].unsqueeze(1).to_broadcast(ALL), ALU.mult))
                    chain.sync()
                    chain(dve.tensor_reduce(a_rec[:, :], mask, AX.X, ALU.max))
                    chain.sync()
                    chain(TT(mask, mask, a_rec[:, :].unsqueeze(2).to_broadcast(ALL), ALU.is_equal))
                    chain.sync()
                    if n == 0:
                        chain(STT(out=a_rest, in0=a_m1, scalar=-3e38, in1=a_logits, op0=ALU.mult, op1=ALU.add))
                        chain.sync()
                        rest = a_rest
                TT(a_m16, a_m1, a_m2, ALU.add).then_inc(a_chosen_ready, 1)

            def pick(out, values, mask):
                chain(TT(a_tmp, values, mask, ALU.mult))
                chain.sync()
                chain(dve.tensor_reduce(out, a_tmp, AX.X, ALU.add))
                chain.sync()

            def a_weights():
                TT(a_e2[:, :], a_v[:, 1, :], a_v[:, 0, :], ALU.subtract).then_inc(a_shift_ready, 1)

            def a_weights_end():
                dve.wait_ge(a_exp_ready, 1)
                dve.wait_ge(tanh_ready, 2)
                chain(TS(a_rec[:, :], a_e2[:, :], 1.0, None, ALU.add))
                chain(TS(tgs[:, :], tg[:, :], 1.0 / WSCALE, None, ALU.mult))
                chain.sync()
                chain(dve.reciprocal(a_rec[:, :], a_rec[:, :]))
                chain.sync()
                chain(TS(a_tw[:, 0, :], a_rec[:, :], tg[:, GX0:GX0 + 1], None, ALU.mult))
                chain.sync()
                chain(TT(a_tw[:, 1, :], a_tw[:, 0, :], a_e2[:, :], ALU.mult))
                chain.sync()

            def a_places():
                counts = ps2[:, 1, 0:NT * E8].rearrange("p (t e) -> p t e", e=E8)
                before = ps2[:, 0, 0:NT * E8].rearrange("p (t e) -> p t e", e=E8)
                dve.wait_ge(a_counts_ready, 1)
                chain(dve.tensor_copy(a_scan0, counts))
                chain.sync()
                src, dst, d = a_scan0, a_scan1, 1
                while d < NT:
                    chain(dve.tensor_copy(dst[:, 0:d, :], src[:, 0:d, :]))
                    chain(TT(dst[:, d:NT, :], src[:, d:NT, :], src[:, 0:NT - d, :], ALU.add))
                    chain.sync()
                    src, dst, d = dst, src, 2 * d
                incl = src
                chain(TT(a_pos, incl, counts, ALU.subtract))
                n, tiles, pad = a_small[:, 0, :], a_small[:, 1, :], a_small[:, 2, :]
                first_tile, start, end_tile = a_small[:, 3, :], a_small[:, 4, :], a_small[:, 5, :]
                yoff = a_small[:, 6, :]
                chain(dve.tensor_copy(n, incl[:, NT - 1, :]))
                chain.sync()
                chain(TT(a_pos, a_pos, before, ALU.add))
                chain(TT(a_tn, n.unsqueeze(2).to_broadcast([P, E8, 16]),
                         iota_f[:, 0:16].unsqueeze(1).to_broadcast([P, E8, 16]), ALU.is_gt))
                chain(TT(a_tg, n.unsqueeze(1).to_broadcast([P, E8, E8]), tri[:, :, :], ALU.mult))
                chain.sync()
                chain(dve.tensor_reduce(tiles, a_tn, AX.X, ALU.add))
                chain(dve.tensor_reduce(start, a_tg, AX.X, ALU.add))
                chain.sync()
                chain(TT(a_tg, tiles.unsqueeze(1).to_broadcast([P, E8, E8]), tri[:, :, :], ALU.mult))
                chain(STT(out=pad, in0=tiles, scalar=float(ROWS), in1=n, op0=ALU.mult, op1=ALU.subtract))
                chain(TT(a_scan0 if incl is a_scan1 else a_scan1, a_pos,
                         start.unsqueeze(1).to_broadcast(ALL), ALU.add))
                chain.sync()
                xpos = a_scan0 if incl is a_scan1 else a_scan1
                chain(dve.tensor_reduce(first_tile, a_tg, AX.X, ALU.add))
                for k, m in enumerate((a_m1, a_m2)):
                    pick(idx_x[:, k, :], xpos, m)
                TS(yoff, first_tile, float(ROWS), None, ALU.mult).then_inc(a_idx_ready, 1)
                dve.wait_ge(a_idx_ready, 1)
                chain(TT(end_tile, first_tile, tiles, ALU.add))
                chain.sync()
                chain(TS(end_tile, end_tile, float(ROWS), None, ALU.mult))

            def a_tables():
                pad, end_row, yoff = a_small[:, 2, :], a_small[:, 5, :], a_small[:, 6, :]
                chain(TT(a_pos, a_pos, yoff.unsqueeze(1).to_broadcast(ALL), ALU.add))
                over = [P, NTILE, E8]
                chain(TT(a_tt, iota_f[:, :].unsqueeze(2).to_broadcast(over),
                         end_row.unsqueeze(1).to_broadcast(over), ALU.is_ge))
                chain.sync()
                chain(dve.tensor_reduce(a_tab[:, 0, :], a_tt, AX.X, ALU.add))
                for k, m in enumerate((a_m1, a_m2)):
                    pick(idx_y[:, k, :], a_pos, m)
                chain(TT(a_tt, a_tt, pad.unsqueeze(1).to_broadcast(over), ALU.mult))
                chain.sync()
                chain(dve.tensor_reduce(a_tab[:, 1, :], a_tt, AX.X, ALU.add))
                chain.sync()
                chain(TT(a_tab[:, 2, :], iota_f[:, :], a_tab[:, 1, :], ALU.subtract))
                chain.sync()
                chain(TS(tile_row[:, :], a_tab[0:1, 2, :], float(T * TOP), None, ALU.min))
                chain(TS(a_tab[0:1, 1, :], a_tab[0:1, 0, :], float(E8 - 1), float(FC * P), ALU.min, ALU.mult))
                chain.sync()
                chain(dve.tensor_copy(tile_column[:, :], a_tab[0:1, 1, :]))
                chain.sync()
                TS(tile_expert[:, :], a_tab[0:1, 0, :], float(E8 - 1), None, ALU.min).then_inc(a_table_ready, 1)

            def a_norm_stats(part):
                tiles = range(STATS[part][0] * JT, STATS[part][1] * JT)
                dve.wait_ge(x_part_loaded[part], 16)
                for j in tiles:
                    chain(dve.bn_stats(a_stats[:, j, :], x_sb[:, j, :]))
                chain.sync()
                for j in tiles:
                    chain(dve.bn_aggr(a_mv[:, j, :], a_stats[:, j, :]))
                chain.sync()
                t = slice(tiles[0], tiles[-1] + 1)
                TS(a_ve[:, t].unsqueeze(2), a_mv[:, t, 1:2], EPS, None, ALU.add).then_inc(a_var_ready, 1)

            def a_norm(c):
                dve.wait_ge(a_rstd_ready, 1 + sum(c >= first for first, _ in STATS[1:]))
                for j in range(JT):
                    t = c * JT + j
                    last = TS(a_xn[:, j, :], x_sb[:, t, :], a_mv[:, t, 0:1], a_rstd[:, t:t + 1],
                              ALU.subtract, ALU.mult)
                last.then_inc(a_xn_ready, 1)
                dve.wait_ge(a_xhi_ready, c + 1)
                TT(a_hl16[:, c % 2, :, P:2 * P], a_xn[:, :, :], a_hl16[:, c % 2, :, 0:P], ALU.subtract)\
                    .then_inc(a_xlo_ready, 1)
                dve.wait_ge(a_xlo_ready, c + 1)

            def hidden_split(k, m):
                dve.wait_ge(a_r_ready, k * FC + FC)
                at_least(dve, a_o_ready, k - 1)
                dve.tensor_copy(a_hh[:, m % 2, :, :], a_r[:, m % 2, :, :]).then_inc(a_hh_ready, 1)
                dve.wait_ge(a_hh_ready, k + 1)
                TT(a_hl[:, m % 2, :, :], a_r[:, m % 2, :, :], a_hh[:, m % 2, :, :], ALU.subtract)\
                    .then_inc(a_hl_ready, 1)

            def result(turn, k, m, expert):
                dve.wait_ge(a_o_ready, k + 1)
                at_least(dve, a_y_stored[m % 2], turn * (16 * PER // 2) + 16 * (m // 2))
                STT(out=a_y[:, m % 2, :, :], in0=ps2[:, m % 2, 0:2 * P].rearrange("p (h d) -> p h d", d=P),
                    scalar=1.0 / WSCALE,
                    in1=b2_bc[:, bass.ds(expert * P, P)].unsqueeze(1).to_broadcast([P, 2, P]),
                    op0=ALU.mult, op1=ALU.add).then_inc(a_y_ready, 1)

            def tile(turn, k, m):
                if is_first(k):
                    hidden_split(0, 0)
                if tile_exists(k + 1):
                    hidden_split(k + 1, m + 1)
                result(turn, k, m, dve.value_load(tile_expert[0:1, bass.ds(k, 1)], min_val=0, max_val=E8 - 1))

            def combine(c):
                for k in range(TOP):
                    dve.wait_ge(a_weighed, TOP * c + (k + 1))
                    if k == 1:
                        dve.wait_ge(a_half_added, c + 1)
                    STT(out=xchunk(c), in0=a_yg[:, k, :, :], scalar=1.0, in1=xchunk(c), op0=ALU.mult,
                        op1=ALU.add).then_inc((a_half_added, a_x_done)[k], 1)

            dve.wait_ge(const_ready, N_CONST)
            a_norm_stats(0)
            a_choose()
            a_places()
            a_norm(0)
            a_weights()
            a_norm_stats(1)
            a_norm(1)
            a_tables()
            split_lo(0)
            split_lo(1)
            for c in range(2, NC):
                a_norm(c)
                split_lo(c)
            a_weights_end()
            dve.wait_ge(small_loaded, 16 * len(SMALL))
            for odd, rows in ((0, slice(0, SEQ)), (1, slice(SEQ, P))):
                src = bv_bc[rows, :].rearrange("p (n o k) -> p n o k", o=2, k=DK)[:, :, odd, :]
                chain(dve.tensor_copy(bv8[rows, :].rearrange("p (b n k) -> p b n k", b=NB, k=DK),
                                      src.unsqueeze(1).to_broadcast([SEQ, NB, HEADS // 2, DK])))
            ternary()
            dve.wait_ge(tern_ready, 2)
            chain.restart()
            run_tiles(dve, tile)

            G4 = JT * GROUPS
            G4 = JT * GROUPS

            def route_groups(c):
                dve.wait_ge(b_score_ready, c + 1)
                chain(TS(b_sc[:, :, :], b_th[:, :].rearrange("p (j e) -> p j e", e=E32), 0.5, 0.5,
                         ALU.mult, ALU.add))
                chain.sync()
                chain(TT(b_scb[:, :, :, :].rearrange("p (j g) a b -> p j (g a b)", j=JT), b_sc[:, :, :],
                         gbias_bc[:, :, :], ALU.add))
                chain.sync()
                a, b = b_scb[:, :, :, 0], b_scb[:, :, :, 1]
                chain(TT(b_mx[:, :, :], a, b, ALU.max))
                chain(TT(b_mn[:, :, :], a, b, ALU.min))
                chain.sync()
                chain(TT(b_t1[:, :], b_mx[:, :, 0], b_mx[:, :, 1], ALU.max))
                chain(TT(b_t2[:, :], b_mx[:, :, 0], b_mx[:, :, 1], ALU.min))
                chain(TT(b_t3[:, :], b_mn[:, :, 0], b_mn[:, :, 1], ALU.max))
                chain.sync()
                chain(TT(b_t2[:, :], b_t2[:, :], b_t3[:, :], ALU.max))
                chain.sync()
                chain(TT(b_gs[:, :, :].rearrange("p j g -> p (j g)"), b_t1[:, :], b_t2[:, :], ALU.add))
                chain.sync()

            def route_mask(c):
                rank8(b_gs[:, :, :])
                chain(TS(b_gm[:, :, :], rk[:, :, :], TOP_GROUPS - 0.5, None, ALU.is_lt))
                chain.sync()
                scb = b_scb[:, :, :, :].rearrange("p g a b -> p g (a b)")
                chain(TT(b_masked[:, :, :].rearrange("p j (g k) -> p (j g) k", k=PER_GROUP), scb,
                         b_gm[:, :, :].rearrange("p j g -> p (j g)").unsqueeze(2).to_broadcast([P, G4, PER_GROUP]),
                         ALU.mult))
                chain.sync()

            def route_top(c):
                for j in range(JT):
                    chain(dve.max(b_m8[:, j, :], b_masked[:, j, :]))
                chain.sync()
                for j in range(JT):
                    chain(dve.match_replace(b_mr[:, j, :], b_m8[:, j, :], b_masked[:, j, :], -3e38))
                chain.sync()
                chain(STT(out=b_ws[:, :, :], in0=b_mr[:, :, :], scalar=-1e38, in1=b_sc[:, :, :], op0=ALU.is_lt,
                          op1=ALU.mult))
                chain.sync()
                chain(dve.tensor_reduce(b_wsum[:, :], b_ws[:, :, :], AX.X, ALU.add))
                chain.sync()
                chain(TS(b_wsum[:, :], b_wsum[:, :], 1e-20, None, ALU.add))
                chain.sync()
                chain(dve.reciprocal(b_wrec[:, :], b_wsum[:, :]))
                chain.sync()
                at_least(dve, b_combT_ready, c)
                TT(b_comb[:, :, :], b_ws[:, :, :], b_wrec[:, :].unsqueeze(2).to_broadcast([P, JT, E32]), ALU.mult)\
                    .then_inc(b_comb_ready, 1)

            def comb_lo(c):
                dve.wait_ge(b_ch_ready, c + 1)
                at_least(dve, b_gu_ready, NP * c)
                STT(out=b_cT[E32:2 * E32, :], in0=ps_misc[0:E32, :], scalar=ROUTED_SCALE, in1=b_cT[0:E32, :],
                    op0=ALU.mult, op1=ALU.subtract).then_inc(b_cl_ready, 1)

            def pair(c, e):
                n = NP * c + e
                dve.wait_ge(b_silu_ready, n + 1)
                dve.wait_ge(b_gu_ready, n + 1)
                TT(b_su[:, e % 2, :], ps4[:, 2 + e % 2, :], b_silu[:, e % 2, :], ALU.mult).then_inc(b_u_used, 1)
                dve.wait_ge(b_u_used, n + 1)
                at_least(dve, b_al_ready, NP * c + max(e - 1, 0))
                TT(b_act[:, e % 2, :], ps2[:, e % 2, :], b_su[:, e % 2, :], ALU.mult).then_inc(b_act_ready, 1)

            def b_update(c):
                dve.wait_ge(b_y_ready, c + 1)
                STT(out=xchunk(c), in0=ps_misc[:, :].rearrange("p (j d) -> p j d", d=P),
                    scalar=tgs[:, GF0:GF0 + 1], in1=xchunk(c), op0=ALU.mult, op1=ALU.add).then_inc(b_x_done, 1)

            def query_lo(c):
                dve.wait_ge(c_q_ready, c + 1)
                at_least(dve, c_s_ready, BP * c)
                TT(c_ql[:, :], c_q[:, :], c_qh[:, :], ALU.subtract).then_inc(c_ql_ready, 1)

            def key_masks(c, step):
                if step == 0:
                    dve.wait_ge(c_k_ready, c + 1)
                    at_least(dve, c_s_ready, BP * c)
                    chain(TT(c_kl[:, :], c_k[:, :], c_kh[:, :], ALU.subtract))
                    for r in range(2):
                        chain(TS(c_km[:, 0, r, :], c_kh[:, :], headmask[:, r:r + 1], None, ALU.mult))
                if step == 1:
                    for r in range(2, 4):
                        chain(TS(c_km[:, 0, r, :], c_kh[:, :], headmask[:, r:r + 1], None, ALU.mult))
                    chain.sync()
                if step == 2:
                    for r in range(4):
                        last = TS(c_km[:, 1, r, :], c_kl[:, :], headmask[:, r:r + 1], None, ALU.mult)
                    last.then_inc(c_km_ready, 1)

            def values(c):
                dve.wait_ge(c_vp_ready, c + 1)
                at_least(dve, c_o_ready, BP * c)
                for odd, rows in ((0, slice(0, SEQ)), (1, slice(SEQ, P))):
                    out = c_vbd[rows, :, :, odd, 0:DK].rearrange("p b n k -> p (b n) k")
                    last = STT(out=out, in0=ps2[rows, 1, :].rearrange("p (n k) -> p n k", k=DK),
                               scalar=1.0 / WSCALE, in1=bv8[rows, :].rearrange("p (n k) -> p n k", k=DK),
                               op0=ALU.mult, op1=ALU.add)
                last.then_inc(c_v_ready, 1)

            def shift(c, p):
                s = ps4[:, :, 0:4 * SEQ].rearrange("p q (r s) -> p q r s", s=SEQ)
                dve.wait_ge(c_s_ready, BP * c + p + 1)
                m = c_max[:, :].rearrange("p (q r) -> p q r", r=4)
                chain(dve.tensor_reduce(m, s, AX.X, ALU.max))
                chain.sync()
                at_least(dve, c_pT_ready, BP * c + p - 1)
                TT(c_p[:, p % 2, :].rearrange("p (q r s) -> p q r s", q=4, r=4), s,
                   m.unsqueeze(3).to_broadcast([P, 4, 4, SEQ]), ALU.subtract).then_inc(c_shift_ready, 1)

            def heads_norm(c, p):
                dve.wait_ge(c_o_ready, BP * c + p + 1)
                o = ps_out[:, 0:HEADS * V9].rearrange("p (h k) -> p h k", k=V9)
                chain(dve.reciprocal(c_rec[:, :].unsqueeze(2), o[:, :, DK:V9]))
                chain.sync()
                if p == 0:
                    at_least(dve, c_oT_ready, c)
                TT(c_on[:, p, :, :], o[:, :, 0:DK], c_rec[:, :].unsqueeze(2).to_broadcast([P, HEADS, DK]),
                   ALU.mult).then_inc(c_on_ready, 1)

            def o_lo(c):
                dve.wait_ge(c_oh_ready, c + 1)
                at_least(dve, c_y_ready, c)
                TT(c_ol[:, :], ps_misc[:, :], c_oh[:, :], ALU.subtract).then_inc(c_ol_ready, 1)

            def c_update(c):
                dve.wait_ge(c_y_ready, c + 1)
                STT(out=c_y[:, :, :], in0=ps_out[:, :].rearrange("p (j d) -> p j d", d=P), scalar=1.0 / WSCALE,
                    in1=bo4[:, :, :], op0=ALU.mult, op1=ALU.add).then_inc(c_y_used, 1)
                dve.wait_ge(c_y_used, c + 1)
                STT(out=xchunk(c), in0=c_y[:, :, :], scalar=tg[:, GX1:GX1 + 1], in1=xchunk(c), op0=ALU.mult,
                    op1=ALU.add).then_inc(c_x_done, 1)

            def d_update(c):
                dve.wait_ge(d_y_ready, c + 1)
                TT(d_y[:, :, :], ps2[:, 0, :].rearrange("p (j d) -> p j d", d=P), fb2_4[:, :, :], ALU.add)\
                    .then_inc(d_y_used, 1)
                dve.wait_ge(d_y_used, c + 1)
                at_least(dve, stored, 16 * c)
                STT(out=x_out[:, :, :], in0=d_y[:, :, :], scalar=tg[:, GF1:GF1 + 1], in1=xchunk(c), op0=ALU.mult,
                    op1=ALU.add).then_inc(d_x_ready, 1)

            combine(0)
            dve.wait_ge(a_x_done, 1)
            norm(nB, 0)
            norm_lo(nB, 0)
            route_groups(0)
            route_mask(0)
            route_top(0)

            def body(i):
                B, C, D = i, i - 1, i - 2
                S = slots(i)
                chain.restart()
                if late_weights(i):
                    comb_lo(B)
                for e in range(NP):
                    if e == S["norm_C"] and has(C):
                        dve.wait_ge(b_x_done, C + 1)
                    if e == S["norm_D"] and has(D):
                        dve.wait_ge(c_x_done, D + 1)
                    if is_first(i) and e == EARLY["norm"]:
                        dve.wait_ge(a_x_done, 2)
                    if has(B + 1) and not is_first(i) and e == S["norm_B"]:
                        dve.wait_ge(a_x_done, B + 2)
                    if has(B):
                        pair(B, e)
                    if is_first(i) and e == EARLY["combine"]:
                        combine(1)
                    if is_first(i) and e == EARLY["norm"]:
                        norm(nB, 1)
                    if has(B + 1) and not is_first(i):
                        if e == S["norm_B"] - 1:
                            combine(B + 1)
                        if e == S["norm_B"]:
                            norm(nB, B + 1)
                    if has(C):
                        if e == S["norm_C"]:
                            norm(nC, C)
                        if e == S["ctx"]:
                            ctx_lo("C", C)
                        if e == S["T_C"]:
                            norm_lo(nC, C)
                        if e == S["q"]:
                            query_lo(C)
                        if S["k"] <= e < S["k"] + 3:
                            key_masks(C, e - S["k"])
                    if has(D):
                        if e == S["norm_D"]:
                            norm(nD, D)
                        if e == S["T_D"]:
                            norm_lo(nD, D)
                if has(C):
                    shift(C, 0)
                    values(C)
                    shift(C, 1)
                if has(B):
                    b_update(B)
                if has(C):
                    shift(C, 2)
                if has(B + 1):
                    norm_lo(nB, B + 1)
                if has(C):
                    heads_norm(C, 0)
                    shift(C, 3)
                if has(B + 1):
                    route_groups(B + 1)
                if has(C):
                    heads_norm(C, 1)
                if has(B + 1):
                    route_mask(B + 1)
                    route_top(B + 1)
                if has(C):
                    heads_norm(C, 2)
                if has(B + 1) and not late_weights(B + 1):
                    comb_lo(B + 1)
                if has(C):
                    heads_norm(C, 3)
                if has(C):
                    o_lo(C)
                if has(D):
                    d_update(D)
                if has(C):
                    c_update(C)

            run_pipeline(dve, body)

        @block.tensor
        def _(pe):
            def split_mm(out, w, x, start=True, stop=True):
                pe.matmul(out, w[0], x[0], start=start, stop=False)
                pe.matmul(out, w[0], x[1], start=False, stop=False)
                return pe.matmul(out, w[1], x[0], start=False, stop=stop)

            def wpart(w, k):
                return w[:, 0, k * P:(k + 1) * P], w[:, 1, k * P:(k + 1) * P]

            def transpose4(out, src):
                for j in range(JT):
                    last = pe.transpose(out[:, j * P:(j + 1) * P], src[:, j, :], ident[:, :])
                return last

            misc = []

            def misc_use(sem_, count):
                if misc:
                    pe.wait_ge(*misc.pop())
                misc.append((sem_, count))

            def norm_T(n, c):
                misc_use(n.lo_ready, c + 1)
                pe.wait_ge(n.xn_ready, c + 1)
                transpose4(ps_misc, n.xn).then_inc(n.xT_ready, 1)

            pe.wait_ge(wg_loaded, 32)
            for half in range(2):
                pe.wait_ge(ctx_loaded[half], 16)
                for t in range(NT // 2):
                    n = half * NT // 2 + t
                    last = pe.matmul(ps_out[:, n * E8:(n + 1) * E8], ctx_half[half][:, t * P:(t + 1) * P],
                                     wg_f32[:, :], start=True, stop=True)
            last.then_inc(a_logit_ready, 1)
            pe.wait_ge(const_ready, N_CONST)
            pe.wait_ge(a_chosen_ready, 1)
            m16 = b_ah[:, 0, 0:NT * E8]
            pe.matmul(ps2[:, 0, 0:NT * E8], below16[:, :], m16, start=True, stop=True)
            pe.matmul(ps2[:, 1, 0:NT * E8], ones16[:, 0:P], m16, start=True, stop=True).then_inc(a_counts_ready, 1)
            pe.wait_ge(tern_abs_ready, 1)
            pe.matmul(ps_misc[:, 0:2], ones[:, :], tern_sum[:, :], start=True, stop=True)\
              .then_inc(tern_total_ready, 1)
            pe.wait_ge(tern_ready, 2)
            pe.wait_ge(split_hi_done, len(JOBS))
            pe.wait_ge(split_lo_done, len(JOBS))

            held = []

            def rows_T(turn, k, m):
                pe.wait_ge(a_rows_loaded[m], turn * 16 + 16)
                at_least(pe, a_xT_ready, k - 1)
                for part in range(2):
                    for h in range(2):
                        last = pe.transpose(T16[m % 2][:, part, h * P:(h + 1) * P],
                                            a_rows[:, m, h, part * P:(part + 1) * P], ident16[:, :])
                last.then_inc(a_T_ready, 1)

            def expert_part(w, part, expert, f):
                return w[:, part, bass.ds(expert + f * P, P)]

            def expert_of(k):
                return pe.value_load(tile_column[0:1, bass.ds(k, 1)], min_val=0, max_val=(E8 - 1) * FC * P)

            def hidden(k, m, expert):
                pe.wait_ge(a_xT_ready, k + 1)
                for f in range(FC):
                    at_least(pe, a_r_ready, (k - 2) * FC + 2 * (f // 2) + 2)
                    w = [expert_part(w1, part, expert, f) for part in range(2)]
                    last = split_mm(h_bank(m, f), w, (a_xT[:, m % 2, 0, :], a_xT[:, m % 2, 1, :]))
                    if f % 2 == 1:
                        last.then_inc(a_h_ready, 1)

            def output(k, m, expert):
                pe.wait_ge(a_hl_ready, k + 1)
                pe.wait_ge(a_hh_ready, k + 1)
                at_least(pe, a_y_ready, k - 1)
                for h in range(2):
                    t = slice(h * P, (h + 1) * P)
                    for f in range(FC):
                        w = [expert_part(w2, part, expert, f) for part in range(2)]
                        last = split_mm(ps2[:, m % 2, t], (a_hh[:, m % 2, f, t], a_hl[:, m % 2, f, t]), w,
                                        start=(f == 0), stop=(f == FC - 1))
                last.then_inc(a_o_ready, 1)

            def tile(turn, k, m):
                if is_first(k):
                    rows_T(0, 0, 0)
                    rows_T(0, 1, 1)
                    held[:] = [expert_of(0)]
                    hidden(0, 0, held[0])
                elif m == 0:
                    held[:] = [expert_of(k)]
                if tile_exists(k + 2):
                    rows_T(turn + (m + 2) // PER, k + 2, (m + 2) % PER)
                if tile_exists(k + 1):
                    held.append(expert_of(k + 1))
                    hidden(k + 1, m + 1, held[1])
                output(k, m, held.pop(0))

            pe.wait_ge(a_table_ready, 1)
            run_tiles(pe, tile)
            misc[:] = [(a_xT_ready, NTILE)]

            def route(c):
                misc_use(b_score_ready, c + 1)
                pe.wait_ge(nB.hi_ready, c + 1)
                pe.wait_ge(nB.lo_ready, c + 1)
                for j in range(JT):
                    t = slice(j * P, (j + 1) * P)
                    out = ps_misc[:, j * E32:(j + 1) * E32]
                    g = wgate[:, 0, E8:E8 + E32], wgate[:, 1, E8:E8 + E32]
                    split_mm(out, (nB.hi[:, t], nB.lo[:, t]), g, stop=False)
                    last = pe.matmul(out, nB.lo[:, t], g[1], start=False, stop=True)
                last.then_inc(b_route_ready, 1)

            def comb_T(c):
                misc_use(b_cl_ready, c + 1)
                pe.wait_ge(b_comb_ready, c + 1)
                for j in range(JT):
                    last = pe.transpose(ps_misc[0:E32, j * P:(j + 1) * P], b_comb[:, j, :], ident[:, :])
                last.then_inc(b_combT_ready, 1)

            def gate_up(c, e):
                x = (nB.hi[:, :], nB.lo[:, :])
                if e == 0:
                    at_least(pe, c_shift_ready, BP * upto(c - 1))
                    at_least(pe, d_gh_ready, FC * upto(c - 2))
                at_least(pe, b_u_used, NP * c + max(e - 1, 0))
                split_mm(ps4[:, e % 2, :], wpart(wgu_g, e), x).then_inc(b_g_ready, 1)
                split_mm(ps4[:, 2 + e % 2, :], wpart(wgu_u, e), x)

            def spread(c, e):
                if e == 0:
                    pe.wait_ge(b_cl_ready, c + 1)
                    at_least(pe, c_pT_copied, BP * upto(c - 1))
                    at_least(pe, d_y_used, upto(c - 2))
                at_least(pe, b_act_ready, NP * c + max(e - 1, 0))
                if e < PAIRS:
                    w = sel[:, e, :, :].rearrange("p a b -> p (a b)")
                    last = pe.matmul(ps2[:, e % 2, :], w, b_cT[:, :], start=True, stop=True)
                else:
                    last = pe.matmul(ps2[:, e % 2, :], unscale16[:, :], ones16[0:1, :], start=True, stop=True)
                last.then_inc(b_gu_ready, 1)

            def down(c, e):
                if e == 0:
                    at_least(pe, c_y_used, upto(c - 1))
                    at_least(pe, b_yT_ready, upto(c))
                pe.wait_ge(b_ah_ready, NP * c + e + 1)
                pe.wait_ge(b_al_ready, NP * c + e + 1)
                split_mm(ps_out[:, :], wpart(wdn, e), (b_ah[:, e % (LAG + 1), :], b_al[:, e % (LAG + 1), :]),
                         start=(e == 0), stop=(e == NP - 1)).then_inc(b_down_done, 1)

            def b_out_T(c):
                misc_use(b_x_done, c + 1)
                pe.wait_ge(b_yT_ready, c + 1)
                for j in range(JT):
                    t = slice(j * P, (j + 1) * P)
                    last = pe.transpose(ps_misc[:, t], b_yT[:, t], ident[:, :])
                last.then_inc(b_y_ready, 1)

            def query(c):
                misc_use(c_q_ready, c + 1)
                pe.wait_ge(nC.hi_ready, c + 1)
                split_mm(ps_misc[:, :], wpart(watt, 0), (nC.hi[:, :], nC.lo[:, :])).then_inc(c_qp_ready, 1)

            def key(c):
                misc_use(c_k_ready, c + 1)
                pe.wait_ge(cx["C"]["hi_ready"], c + 1)
                pe.wait_ge(cx["C"]["lo_ready"], c + 1)
                split_mm(ps_misc[:, :], wpart(watt, 1), (cx["C"]["hi"][:, :], cx["C"]["lo"][:, :]))\
                    .then_inc(c_kp_ready, 1)

            def values(c, i):
                at_least(pe, b_act_ready, NP * upto(i + 1))
                for b in range(NB):
                    t = slice(b * SEQ, (b + 1) * SEQ)
                    for odd in range(2):
                        out = ps2[odd * SEQ:odd * SEQ + SEQ, 1, b * SEQ:(b + 1) * SEQ]
                        w = [watt[:, part, 2 * P:3 * P].rearrange("p (n o k) -> p n o k", o=2, k=DK)[:, :, odd, :]
                             for part in range(2)]
                        last = split_mm(out, (cx["C"]["hi"][:, t], cx["C"]["lo"][:, t]), w)
                last.then_inc(c_vp_ready, 1)

            def scores(c, i, p):
                if p == 0:
                    for s in (c_q_ready, c_ql_ready, c_km_ready):
                        pe.wait_ge(s, c + 1)
                    at_least(pe, b_u_used, NP * upto(i + 1))
                    at_least(pe, d_gh_ready, FC * upto(i - 2))
                at_least(pe, c_shift_ready, BP * c + p)
                for half in range(2):
                    t = slice((2 * p + half) * SEQ, (2 * p + half + 1) * SEQ)
                    for q in range(4):
                        rows = slice(32 * q, 32 * q + 32)
                        out = ps4[half * SEQ:half * SEQ + SEQ, q, 0:4 * SEQ]
                        last = split_mm(out, (c_qh[rows, t], c_ql[rows, t]),
                                        (c_km[rows, 0, :, t], c_km[rows, 1, :, t]))
                last.then_inc(c_s_ready, 1)

            def probs_T(c, i, p):
                pe.wait_ge(c_exp_ready, BP * c + p + 1)
                if p == 0:
                    pe.wait_ge(c_v_ready, c + 1)
                at_least(pe, c_pT_copied, BP * c + p)
                for h in range(HEADS // 2):
                    last = pe.transpose(ps2[:, h // 4, (h % 4) * P:(h % 4 + 1) * P],
                                        c_p[:, p % 2, h * P:(h + 1) * P], ident[:, :])
                last.then_inc(c_pT_ready, 1)

            def weighted(c, i, p):
                pe.wait_ge(c_pT_copied, BP * c + p + 1)
                if p == 0:
                    pe.wait_ge(c_v_ready, c + 1)
                    at_least(pe, b_yT_ready, upto(i + 1))
                at_least(pe, c_on_ready, BP * c + p)
                for half in range(2):
                    for h in range(HEADS // 2):
                        o = h * 2 * V9
                        last = pe.matmul(ps_out[half * SEQ:half * SEQ + SEQ, o:o + 2 * V9],
                                         c_pT[:, p % 2, h, half * SEQ:half * SEQ + SEQ],
                                         c_vbd[:, 2 * p + half, h, :, :].rearrange("p a b -> p (a b)"),
                                         start=True, stop=True)
                last.then_inc(c_o_ready, 1)

            def o_T(c):
                misc_use(c_ol_ready, c + 1)
                pe.wait_ge(c_on_ready, BP * (c + 1))
                for j in range(JT):
                    last = pe.transpose(ps_misc[:, j * P:(j + 1) * P],
                                        c_on[:, j, :, :].rearrange("p h k -> p (h k)"), ident[:, :])
                last.then_inc(c_oT_ready, 1)

            def project(c):
                pe.wait_ge(c_oh_ready, c + 1)
                pe.wait_ge(c_ol_ready, c + 1)
                for j in range(JT):
                    t = slice(j * P, (j + 1) * P)
                    last = split_mm(ps_out[:, t], (c_oh[:, t], c_ol[:, t]), wpart(watt, 3))
                last.then_inc(c_y_ready, 1)

            def d_hidden(c, i, part):
                if part == 0:
                    pe.wait_ge(nD.hi_ready, c + 1)
                    pe.wait_ge(nD.lo_ready, c + 1)
                    at_least(pe, c_shift_ready, BP * upto(i))
                    at_least(pe, b_u_used, NP * upto(i + 1))
                    at_least(pe, d_gh_ready, FC * c)
                for k in (2 * part, 2 * part + 1):
                    w = wt1[:, k * P:(k + 1) * P]
                    pe.matmul(ps4[:, k, :], w, nD.hi[:, :], start=True, stop=False)
                    pe.matmul(ps4[:, k, :], w, nD.lo[:, :], start=False, stop=True).then_inc(d_h_ready, 1)

            def d_out(c, i):
                pe.wait_ge(d_gl_ready, FC * (c + 1))
                at_least(pe, c_pT_copied, BP * upto(i))
                at_least(pe, b_act_ready, NP * upto(i + 1))
                at_least(pe, d_y_used, c)
                for j in range(JT):
                    t = slice(j * P, (j + 1) * P)
                    for k in range(FC):
                        w = wt2[:, k * P:(k + 1) * P]
                        pe.matmul(ps2[:, 0, t], d_gh[:, k, t], w, start=(k == 0), stop=False)
                        last = pe.matmul(ps2[:, 0, t], d_gl[:, k, t], w, start=False, stop=(k == FC - 1))
                last.then_inc(d_y_ready, 1)

            norm_T(nB, 0)
            route(0)

            def body(i):
                B, C, D = i, i - 1, i - 2
                S = slots(i)
                if not isinstance(i, int):
                    misc[:] = [(c_ol_ready, i - 1)]
                for e in range(NP):
                    if has(C):
                        if e == S["T_C"]:
                            norm_T(nC, C)
                        if e == S["q"]:
                            query(C)
                        if e == S["k"]:
                            key(C)
                    if e == S["T_D"] and has(D):
                        norm_T(nD, D)
                    if late_weights(i) and e < 2:
                        if e == 1:
                            gate_up(B, 0)
                            gate_up(B, 1)
                            comb_T(B)
                            spread(B, 0)
                            spread(B, 1)
                    elif has(B):
                        gate_up(B, e)
                        spread(B, e)
                        if e >= LAG:
                            down(B, e - LAG)
                if has(B):
                    down(B, NP - 3)
                if has(C):
                    scores(C, i, 0)
                if has(B):
                    down(B, NP - 2)
                if has(C):
                    values(C, i)
                if has(B):
                    down(B, NP - 1)
                if has(C):
                    scores(C, i, 1)
                if has(B):
                    b_out_T(B)
                if has(C):
                    probs_T(C, i, 0)
                    scores(C, i, 2)
                if has(B + 1):
                    norm_T(nB, B + 1)
                if has(C):
                    probs_T(C, i, 1)
                    weighted(C, i, 0)
                if has(B + 1):
                    route(B + 1)
                if has(C):
                    scores(C, i, 3)
                    probs_T(C, i, 2)
                    weighted(C, i, 1)
                    probs_T(C, i, 3)
                if has(D):
                    d_hidden(D, i, 0)
                if has(C):
                    weighted(C, i, 2)
                if has(D):
                    d_hidden(D, i, 1)
                if has(B + 1) and not late_weights(B + 1):
                    comb_T(B + 1)
                if has(C):
                    weighted(C, i, 3)
                    o_T(C)
                if has(D):
                    d_out(D, i)
                if has(C):
                    project(C)

            for i in range(LOOP[0]):
                body(i)
            with pe.Fori(*LOOP) as i:
                body(i)
            misc[:] = [(c_ol_ready, LOOP[1] - 1)]
            for i in range(LOOP[1], NC + 2):
                body(i)


def kernel(**inputs):
    import numpy as np
    import concourse.bacc as bacc
    from concourse import mybir as mb
    from concourse.bass_utils import run_bass_kernel_spmd

    a = {k: np.asarray(v) for k, v in inputs.items()}
    T = a["x"].shape[0] * a["x"].shape[1]

    def col(v):
        return v.reshape(-1, 1)

    def parts(v, n):
        return v.reshape(n, P, -1).transpose(1, 0, 2).reshape(P, -1)

    w1, w2 = a["L0_xattn_W1"], a["L0_xattn_W2"]
    arrays = {
        "x": a["x"].reshape(T, P),
        "ctxT": a["ctx_1024"].reshape(T, P).T,
        "g_xattn": a["g_xattn"], "g_ffn": a["g_ffn"],
        "a_wg": a["L0_xattn_Wg"], "a_bg": a["L0_xattn_bg"],
        "a_w1": w1.transpose(1, 0, 2).reshape(P, -1),
        "a_b1": a["L0_xattn_b1"].reshape(-1, P).T,
        "a_w2": parts(w2.reshape(-1, P), w2.shape[0] * w2.shape[1] // P),
        "a_b2": a["L0_xattn_b2"].reshape(-1),
        "b_gate_w": a["L0_ffn_gate_w"].T, "b_gate_bias": a["L0_ffn_gate_bias"],
        "b_w_gate": a["L0_ffn_w_gate"].reshape(-1, P).T,
        "b_w_up": a["L0_ffn_w_up"].reshape(-1, P).T,
        "b_w_down": parts(a["L0_ffn_w_down"].transpose(0, 2, 1).reshape(-1, P), 16),
        "b_sh_gate": a["L0_ffn_sh_gate"].T, "b_sh_up": a["L0_ffn_sh_up"].T, "b_sh_down": a["L0_ffn_sh_down"].T,
        "c_wq": a["L1_xattn_W_Q"], "c_bq": col(a["L1_xattn_b_Q"]),
        "c_wk": a["L1_xattn_W_K"], "c_bk": col(a["L1_xattn_b_K"]),
        "c_wv": a["L1_xattn_W_V"], "c_bv": a["L1_xattn_b_V"],
        "c_wo": a["L1_xattn_W_O"], "c_bo": a["L1_xattn_b_O"],
        "d_w1": a["L1_ffn_W1"].T, "d_b1": a["L1_ffn_b1"].reshape(-1, P).T,
        "d_w2": parts(a["L1_ffn_W2"].T, 4), "d_b2": a["L1_ffn_b2"],
    }
    arrays = {k: np.ascontiguousarray(v) for k, v in arrays.items()}
    nc = bacc.Bacc("TRN2", target_bir_lowering=False, num_devices=1)
    args = [nc.dram_tensor(k, v.shape, mb.dt.from_np(v.dtype), kind="ExternalInput").ap()
            for k, v in arrays.items()]
    args.append(nc.dram_tensor("out", (T, P), mb.dt.float32, kind="ExternalOutput").ap())
    build_flamingo(nc, *args)
    r = run_bass_kernel_spmd(nc, [arrays], core_ids=[0])
    return r.results[0]["out"].reshape(a["x"].shape)
```
